# Optimizing a Trainium2 kernel written in Bass

```python
import numpy as np
import jax
import jax.numpy as jnp

def _softmax(x, axis=-1):
    return jax.nn.softmax(x, axis=axis)

def _gelu(x):
    return jax.nn.gelu(x, approximate=True)

def _silu(x):
    return jax.nn.silu(x)

def _sigmoid(x):
    return jax.nn.sigmoid(x)

def _layernorm(x, axis=-1, eps=1e-05):
    m = jnp.mean(x, axis=axis, keepdims=True)
    v = jnp.var(x, axis=axis, keepdims=True)
    return (x - m) / jnp.sqrt(v + eps)

def _scatter_add(tgt, idx, src, axis=0):
    return tgt.at[idx].add(src)

def _segment_sum(src, seg, n):
    return jax.ops.segment_sum(src, seg, n)
kernel_name = 'mk_gnn_resnorm_d1_gnn_r8_91923a'

def setup_inputs(seed: int=0):
    np.random.seed(seed)
    _w = jnp.asarray

    def _rec_inputs():
        import jax
        import jax.numpy as jnp
        _gk = jax.random.key(seed)
        x = -0.000202 + 1 * jax.random.normal(jax.random.fold_in(_gk, 1), (12500, 64), jnp.float32)
        _s = jax.random.randint(jax.random.fold_in(_gk, 2), (100000,), 0, 12500, jnp.int32)
        _d = jax.random.randint(jax.random.fold_in(_gk, 3), (100000,), 0, 12500, jnp.int32)
        _loop = jnp.arange(12500, dtype=jnp.int32)
        src = jnp.concatenate([_s, _d, _loop])
        dst = jnp.concatenate([_d, _s, _loop])
        _o = jnp.argsort(dst, stable=True)
        src = src[_o]
        dst = dst[_o]
        edge_attr_16 = 0.000283511 + 1.00007 * jax.random.normal(jax.random.fold_in(_gk, 11), (212500, 16), jnp.float32)
        return (x, src, dst, edge_attr_16)
    x, src, dst, edge_attr_16 = _rec_inputs()

    def _L0_gnn_setup():
        import jax, jax.numpy as jnp
        import numpy as np
        N_NODES = 12500
        N_EDGES = 150000
        HID = 64
        EDGE_DIM = 16
        N_LAYERS = 3

        def _gru_cell(x, h, Wih, Whh, bih, bhh):
            gi = x @ Wih + bih
            gh = h @ Whh + bhh
            gi_r, gi_z, gi_n = jnp.split(gi, 3, axis=-1)
            gh_r, gh_z, gh_n = jnp.split(gh, 3, axis=-1)
            r = jax.nn.sigmoid(gi_r + gh_r)
            z = jax.nn.sigmoid(gi_z + gh_z)
            n = jnp.tanh(gi_n + r * gh_n)
            return (1.0 - z) * n + z * h
        key = jax.random.key(seed)
        ks = jax.random.split(key, 16)
        s = 0.1
        return {'node_features': jax.random.normal(ks[0], (N_NODES, HID), jnp.float32), 'edge_index': jax.random.randint(ks[1], (2, N_EDGES), 0, N_NODES, jnp.int32), 'edge_features': jax.random.normal(ks[2], (N_EDGES, EDGE_DIM), jnp.float32), 'enc_W': jax.random.normal(ks[3], (HID, HID), jnp.float32) * s, 'enc_b': jnp.zeros((HID,), jnp.float32), 'msg_W1': jax.random.normal(ks[4], (N_LAYERS, 2 * HID + EDGE_DIM, HID), jnp.float32) * s, 'msg_b1': jnp.zeros((N_LAYERS, HID), jnp.float32), 'msg_W2': jax.random.normal(ks[5], (N_LAYERS, HID, HID), jnp.float32) * s, 'msg_b2': jnp.zeros((N_LAYERS, HID), jnp.float32), 'gru_Wih': jax.random.normal(ks[6], (N_LAYERS, HID, 3 * HID), jnp.float32) * s, 'gru_Whh': jax.random.normal(ks[7], (N_LAYERS, HID, 3 * HID), jnp.float32) * s, 'gru_bih': jnp.zeros((N_LAYERS, 3 * HID), jnp.float32), 'gru_bhh': jnp.zeros((N_LAYERS, 3 * HID), jnp.float32), 'ro_W1': jax.random.normal(ks[8], (HID, HID), jnp.float32) * s, 'ro_b1': jnp.zeros((HID,), jnp.float32), 'ro_W2': jax.random.normal(ks[9], (HID, HID), jnp.float32) * s, 'ro_b2': jnp.zeros((HID,), jnp.float32)}
    _L0_gnn_all = _L0_gnn_setup()
    _L0_gnn_in = {k: v for k, v in _L0_gnn_all.items() if k in ('enc_W', 'enc_b', 'msg_W1', 'msg_b1', 'msg_W2', 'msg_b2', 'gru_Wih', 'gru_Whh', 'gru_bih', 'gru_bhh', 'ro_W1', 'ro_b1', 'ro_W2', 'ro_b2')}
    del _L0_gnn_all
    return {'x': x, 'src': src, 'dst': dst, 'edge_attr_16': edge_attr_16, 'L0_gnn_enc_W': _L0_gnn_in['enc_W'], 'L0_gnn_enc_b': _L0_gnn_in['enc_b'], 'L0_gnn_msg_W1': _L0_gnn_in['msg_W1'], 'L0_gnn_msg_b1': _L0_gnn_in['msg_b1'], 'L0_gnn_msg_W2': _L0_gnn_in['msg_W2'], 'L0_gnn_msg_b2': _L0_gnn_in['msg_b2'], 'L0_gnn_gru_Wih': _L0_gnn_in['gru_Wih'], 'L0_gnn_gru_Whh': _L0_gnn_in['gru_Whh'], 'L0_gnn_gru_bih': _L0_gnn_in['gru_bih'], 'L0_gnn_gru_bhh': _L0_gnn_in['gru_bhh'], 'L0_gnn_ro_W1': _L0_gnn_in['ro_W1'], 'L0_gnn_ro_b1': _L0_gnn_in['ro_b1'], 'L0_gnn_ro_W2': _L0_gnn_in['ro_W2'], 'L0_gnn_ro_b2': _L0_gnn_in['ro_b2']}

def reference(x, src, dst, edge_attr_16, L0_gnn_enc_W, L0_gnn_enc_b, L0_gnn_msg_W1, L0_gnn_msg_b1, L0_gnn_msg_W2, L0_gnn_msg_b2, L0_gnn_gru_Wih, L0_gnn_gru_Whh, L0_gnn_gru_bih, L0_gnn_gru_bhh, L0_gnn_ro_W1, L0_gnn_ro_b1, L0_gnn_ro_W2, L0_gnn_ro_b2):
    import jax
    import jax.numpy as jnp

    def _L0_gnn_ref(node_features, edge_index, edge_features, enc_W, enc_b, msg_W1, msg_b1, msg_W2, msg_b2, gru_Wih, gru_Whh, gru_bih, gru_bhh, ro_W1, ro_b1, ro_W2, ro_b2):
        import jax, jax.numpy as jnp
        import numpy as np
        N_NODES = 12500
        N_EDGES = 150000
        HID = 64
        EDGE_DIM = 16
        N_LAYERS = 3

        def _gru_cell(x, h, Wih, Whh, bih, bhh):
            gi = x @ Wih + bih
            gh = h @ Whh + bhh
            gi_r, gi_z, gi_n = jnp.split(gi, 3, axis=-1)
            gh_r, gh_z, gh_n = jnp.split(gh, 3, axis=-1)
            r = jax.nn.sigmoid(gi_r + gh_r)
            z = jax.nn.sigmoid(gi_z + gh_z)
            n = jnp.tanh(gi_n + r * gh_n)
            return (1.0 - z) * n + z * h
        src, dst = (edge_index[0], edge_index[1])
        n_nodes = node_features.shape[0]
        h = node_features @ enc_W + enc_b
        for l in range(N_LAYERS):
            cat = jnp.concatenate([h[src], h[dst], edge_features], axis=-1)
            m = jax.nn.relu(cat @ msg_W1[l] + msg_b1[l]) @ msg_W2[l] + msg_b2[l]
            agg = jax.ops.segment_sum(m, dst, num_segments=n_nodes)
            h = _gru_cell(agg, h, gru_Wih[l], gru_Whh[l], gru_bih[l], gru_bhh[l])
        return jax.nn.relu(h @ ro_W1 + ro_b1) @ ro_W2 + ro_b2
    edge_index = jnp.stack([src, dst])
    x = _layernorm(x + _L0_gnn_ref(x, edge_index, edge_attr_16, L0_gnn_enc_W, L0_gnn_enc_b, L0_gnn_msg_W1, L0_gnn_msg_b1, L0_gnn_msg_W2, L0_gnn_msg_b2, L0_gnn_gru_Wih, L0_gnn_gru_Whh, L0_gnn_gru_bih, L0_gnn_gru_bhh, L0_gnn_ro_W1, L0_gnn_ro_b1, L0_gnn_ro_W2, L0_gnn_ro_b2), axis=-1)
    return x

_drawn_inputs = setup_inputs


def setup_inputs(seed=0):
    import zlib

    import numpy as np

    out = dict(_drawn_inputs(seed))
    spreads = {'L0_gnn_enc_b': (0.0, 0.1),
     'L0_gnn_msg_b1': (0.0, 0.1),
     'L0_gnn_msg_b2': (0.0, 0.1),
     'L0_gnn_gru_bih': (0.0, 0.298),
     'L0_gnn_gru_bhh': (0.0, 0.375),
     'L0_gnn_ro_b1': (0.0, 0.1),
     'L0_gnn_ro_b2': (0.0, 0.1)}
    factors = {}
    for name, (base, spread) in spreads.items():
        noise = np.random.default_rng([zlib.crc32(name.encode()), seed]).standard_normal(out[name].shape)
        drawn = base * np.exp(spread * noise) if base else spread * noise
        out[name] = jnp.asarray(drawn.astype(out[name].dtype))
    for name, factor in factors.items():
        out[name] = (out[name] * factor).astype(out[name].dtype)
    return out
```

```python
import concourse.bass as bass
from concourse import mybir
from contextlib import ExitStack

F32 = mybir.dt.float32
BF16 = mybir.dt.bfloat16
I32 = mybir.dt.int32
U32 = mybir.dt.uint32
ALU = mybir.AluOpType
ACT = mybir.ActivationFunctionType
AX = mybir.AxisListType

LAYERS = 3
HID = 64
EDGE_DIM = 16
NODES = 12500
EDGES = 212500
EDGE_TILES = 8
STEP = EDGE_TILES * 128
STEPS = -(-EDGES // STEP)
WINDOW = 96
FEATS = WINDOW + EDGE_DIM
KEDGE = FEATS + 1
LOOP_STEPS = 8
LOOPS = STEPS // LOOP_STEPS
CHUNK = 448
CPART = CHUNK // 4
CHUNKS = -(-NODES // CHUNK)
LOOPED = LOOPS - 1
NPAD = CHUNKS * CHUNK
NWIN = NPAD + WINDOW
MAX_PASSES = NODES // WINDOW + 1
LAST_PART = (NODES - (CHUNKS - 1) * CHUNK) // 4
GATHER_SLOTS = 4
CREDIT = GATHER_SLOTS
ENC_SLOT = CHUNKS // 2
GRU_OPS = 6
NORM_OPS = 9
EPS = 1e-5


def build(nc, io):
    with ExitStack() as ctx:
        def sb(name, shape, dt=F32):
            return ctx.enter_context(nc.sbuf_tensor(name, shape, dt))

        def sem(name):
            return ctx.enter_context(nc.semaphore(name))

        p_tab = [nc.dram_tensor(f"p_tab{l}", [NPAD, HID], F32).ap() for l in range(LAYERS)]
        q_tab = [nc.dram_tensor(f"q_tab{l}", [NWIN, HID], F32).ap() for l in range(LAYERS)]
        range_tab = nc.dram_tensor("range_tab", [2, STEPS], F32).ap()

        ident = sb("ident", [128, 128], BF16)
        zeros = sb("zeros", [128, CHUNK])
        iota_i = sb("iota_i", [128, WINDOW], I32)
        stair_i = sb("stair_i", [1, STEPS], I32)
        stair = sb("stair", [1, STEPS])
        rungs_i = sb("rungs_i", [1, MAX_PASSES], I32)
        rungs = sb("rungs", [1, MAX_PASSES])
        enc_w = sb("enc_w", [HID, HID])
        enc_b = sb("enc_b", [128, 1])
        w1_nodes = sb("w1_nodes", [128, LAYERS, 2 * HID])
        w2t_b2 = sb("w2t_b2", [HID, LAYERS, HID + 1])
        wih = sb("wih", [HID, LAYERS, 3 * HID])
        gate_w = sb("gate_w", [128, LAYERS, 4 * HID])
        deg_w = sb("deg_w", [128, LAYERS, 4 * HID])
        bias_zr = sb("bias_zr", [128, LAYERS])
        bias_hzr = sb("bias_hzr", [128, LAYERS])
        bias_in = sb("bias_in", [HID, LAYERS])
        bias_hn = sb("bias_hn", [128, LAYERS])
        ro_w1 = sb("ro_w1", [128, HID])
        ro_b1 = sb("ro_b1", [HID, 1])
        ro_w2b = sb("ro_w2b", [HID + 1, HID])
        low_high = sb("low_high", [STEPS // 2, 2, 2])
        dst_i = sb("dst_i", [128, STEPS, EDGE_TILES], I32)
        base_all = sb("base_all", [128, STEPS])
        rel = sb("rel", [128, STEPS, EDGE_TILES])
        base_f = sb("base_f", [1, STEPS])
        high_f = sb("high_f", [1, STEPS])
        spread = sb("spread", [1, STEPS])
        late = sb("late", [1, STEPS])
        start_f = sb("start_f", [1, STEPS])
        base_i = sb("base_i", [1, STEPS], I32)
        widest = sb("widest", [1, 1])
        reach = sb("reach", [1, MAX_PASSES])
        passes_f = sb("passes_f", [1, 1])
        late_n = sb("late_n", [1, 1])
        slow_f = sb("slow_f", [1, 1])
        flags = sb("flags", [1, 2], I32)
        state = sb("state", [128, NWIN])
        degree = sb("degree", [128, NWIN])
        dst_steps = degree[0:STEPS // 2, 0:2 * STEP].bitcast(I32).rearrange("p (j e) -> p j e", j=2)
        idx = [sb(f"idx{s}", [128, EDGE_TILES], U32) for s in range(GATHER_SLOTS)]
        p_src = [sb(f"p_src{s}", [128, EDGE_TILES, HID]) for s in range(GATHER_SLOTS)]
        hot_t = [sb(f"hot_t{s}", [128, EDGE_TILES, WINDOW], BF16) for s in range(2)]
        hot = [sb(f"hot{s}", [128, EDGE_TILES, WINDOW]) for s in range(2)]
        pick = [sb(f"pick{s}", [128, STEP]) for s in range(2)]
        source = sb("source", [128, LAYERS, 2, HID])
        pre = [sb(f"pre{s}", [128, EDGE_TILES, HID]) for s in range(2)]
        msg = [sb(f"msg{s}", [128, EDGE_TILES, HID + 1]) for s in range(2)]
        x_t = [sb(f"x_t{s}", [HID, CHUNK]) for s in range(2)]
        h_enc = [sb(f"h_enc{s}", [128, CHUNK]) for s in range(2)]
        chunk = sb("chunk", [128, CHUNK])
        chunk_deg = sb("chunk_deg", [128, CHUNK])
        zr = sb("zr", [128, CHUNK])
        rn = sb("rn", [HID, CHUNK])
        npre = sb("npre", [HID, CHUNK])
        n_hi = sb("n_hi", [128, CHUNK])
        diff = sb("diff", [HID, CHUNK])
        zdiff = sb("zdiff", [128, CHUNK])
        h_next = sb("h_next", [128, CHUNK])
        stage = [sb(f"stage{s}", [CPART, 2, 4, HID]) for s in range(2)]
        hid = sb("hid", [HID + 1, CHUNK])
        x_rows = sb("x_rows", [CPART, 4, HID])
        y = sb("y", [CPART, 4, HID])
        yc = sb("yc", [CPART, 4, HID])
        ysq = sb("ysq", [CPART, 4, HID])
        ysum = sb("ysum", [CPART, 4])
        ymean = sb("ymean", [CPART, 4])
        vsum = sb("vsum", [CPART, 4])
        veps = sb("veps", [CPART, 4])
        sd = sb("sd", [CPART, 4])
        rstd = sb("rstd", [CPART, 4])
        y_out = sb("y_out", [CPART, 4, HID])

        bank = [ctx.enter_context(nc.psum_tensor(f"bank{i}", [128, 512], F32)) for i in range(5)]
        iota_ps = bank[0][:, 0:WINDOW]
        sum_ps = bank[1]
        zr_ps, n_ps, pq_ps = bank[2], bank[3], bank[4]
        hott_ps = ctx.enter_context(nc.psum_tensor("hott_ps", [128, STEP], BF16))
        pre_ps = [ctx.enter_context(nc.psum_tensor(f"pre_ps{s}", [128, EDGE_TILES, HID], F32)) for s in range(2)]

        consts = sem("consts")
        dst_in = sem("dst_in")
        steps_in = sem("steps_in")
        weights_in = sem("weights_in")
        reduced = sem("reduced")
        range_out = sem("range_out")
        range_in = sem("range_in")
        setup = sem("setup")
        vw_ps = sem("vw_ps")
        vw_sb = sem("vw_sb")
        zero_rows = sem("zero_rows")
        cleared = sem("cleared")
        bias_ready = sem("bias_ready")
        xt_in = [sem(f"xt_in{s}") for s in range(2)]
        enc_in = sem("enc_in")
        enc_ps = sem("enc_ps")
        enc_h = sem("enc_h")
        enc_kept = sem("enc_kept")
        enc_projected = sem("enc_projected")
        enc_staged = sem("enc_staged")
        stored = [sem(f"stored{s}") for s in range(2)]
        idx_in = [sem(f"idx_in{s}") for s in range(GATHER_SLOTS)]
        edge_in = [sem(f"edge_in{s}") for s in range(2)]
        pace = sem("pace")
        gathered = [sem(f"gathered{s}") for s in range(GATHER_SLOTS)]
        hot_t_ready = sem("hot_t_ready")
        hot_ready = sem("hot_ready")
        flipped = sem("flipped")
        pick_ready = sem("pick_ready")
        combined = sem("combined")
        added = sem("added")
        msg_ready = sem("msg_ready")
        scattered = sem("scattered")
        summed = sem("summed")
        windows = sem("windows")
        window_step = sem("window_step")
        pass_read = sem("pass_read")
        chunk_in = sem("chunk_in")
        gates_ps = sem("gates_ps")
        zr_ready = sem("zr_ready")
        gru = sem("gru")
        n_ready = sem("n_ready")
        h_kept = sem("h_kept")
        projected = sem("projected")
        staged = sem("staged")
        hid_ps = sem("hid_ps")
        hid_ready = sem("hid_ready")
        y_ps = sem("y_ps")
        xr_in = sem("xr_in")
        norm = sem("norm")
        sd_ready = sem("sd_ready")
        out_done = sem("out_done")

        def done(k):
            return k + (CREDIT + 1)

        def slot_free(k, slots=2):
            return k + (CREDIT + 1 - slots)

        def single_free(k):
            return k + CREDIT

        def arrivals(k, s, each, slots=2):
            return (k - s) * (each // slots) + each

        def cols(c):
            return bass.ds(c * CHUNK, CHUNK)

        def before(l, c):
            return c + l * CHUNKS

        def stored_before(l, c, s):
            if s == 0:
                return 32 * (min(c, LOOPED) + ENC_SLOT + (LOOPED + 1) * l if isinstance(c, int)
                             else c + (ENC_SLOT + (LOOPED + 1) * l))
            return 32 * (ENC_SLOT + 2 * l + (c - LOOPED) // 2)

        def all_stored(eng, l):
            eng.wait_ge(stored[0], 32 * (ENC_SLOT + (LOOPED + 1) * l))
            eng.wait_ge(stored[1], 32 * (ENC_SLOT + 2 * l))

        def settle(eng):
            eng.sem_inc(pace, 1)

        def load_flags(eng):
            eng.wait_ge(windows, 1)
            return (eng.value_load(flags[0:1, 0:1], min_val=1, max_val=MAX_PASSES),
                    eng.value_load(flags[0:1, 1:2], min_val=0, max_val=STEPS + MAX_PASSES))

        def run_layer(eng, l, passes, slow, lead=None, front=None, back=None, chunk_stage=None, end_pass=None,
                      end_passes=None):
            k0 = 0 if l == 0 else passes * (l * STEPS)
            last = k0 + passes * STEPS - 1

            def part(what, i, k, j):
                if what:
                    what(l, i * LOOP_STEPS + j, k + i * LOOP_STEPS + j, j % GATHER_SLOTS)

            def round_of_steps(i, k, with_chunk, final=False):
                for j in range(LOOP_STEPS):
                    if j + 2 < LOOP_STEPS or not final:
                        part(lead, i, k, j + 2)
                    if j + 1 < LOOP_STEPS or not final:
                        part(front, i, k, j + 1)
                    part(back, i, k, j)
                    if with_chunk and chunk_stage:
                        chunk_stage(l, j, i - 1, 0, k + i * LOOP_STEPS - 1)

            def first_parts(k):
                part(lead, 0, k, 0)
                part(lead, 0, k, 1)
                part(front, 0, k, 0)

            with eng.If(slow == 0):
                first_parts(k0)
                round_of_steps(0, k0, False)
                with eng.Fori(1, LOOPS - 1) as i:
                    round_of_steps(i, k0, True)
                round_of_steps(LOOPS - 1, k0, True, True)
            with eng.Else():
                with eng.Fori(0, passes) as w:
                    first_parts(k0 + w * STEPS)
                    with eng.Fori(0, LOOPS - 1) as i:
                        round_of_steps(i, k0 + w * STEPS, False)
                    round_of_steps(LOOPS - 1, k0 + w * STEPS, False, True)
                    if end_pass:
                        end_pass(l, w, k0 + w * STEPS + (STEPS - 1))
                if end_passes:
                    end_passes(l)
                if chunk_stage:
                    with eng.Fori(0, LOOPED) as c:
                        for j in range(LOOP_STEPS):
                            chunk_stage(l, j, c, 0, last)
            if chunk_stage:
                for c in range(LOOPED, CHUNKS):
                    for j in range(LOOP_STEPS):
                        chunk_stage(l, j, c, c % 2, last)

        def chunk_rows(table, c):
            rows = table.rearrange("(c p j) f -> c p j f", p=CPART, j=4)
            return rows[bass.ds(c, 1)].rearrange("o p j f -> (o p) j f")

        enc_h_ps = [zr_ps, n_ps]
        enc_pq_ps = [pq_ps, sum_ps]

        def pq_view(ps):
            return ps[0:CPART, :].rearrange("p (j t f) -> p j t f", j=4, t=2)

        block = ctx.enter_context(nc.Block())

        @block.sync
        def _(sp):
            sp.dma_start(enc_w[:], io["enc_W"]).then_inc(enc_in, 16)
            sp.dma_start(enc_b[HID:128, :], io["enc_b"]).then_inc(enc_in, 16)
            sp.dma_start(w1_nodes[HID:128], io["w1_nodes"]).then_inc(enc_in, 16)
            for s in range(2):
                sp.dma_start(x_t[s][:], io["x_t"][s]).then_inc(xt_in[s], 16)
            sp.dma_start(dst_steps, io["dst_steps"]).then_inc(steps_in, 16)
            sp.dma_start(dst_i[:], io["dst"]).then_inc(dst_in, 16)
            sp.dma_start(w2t_b2[:], io["w2t_b2"]).then_inc(weights_in, 16)
            sp.dma_start(wih[:], io["wih"]).then_inc(weights_in, 16)
            sp.wait_ge(reduced, 1)
            with nc.allow_non_contiguous_dma(reason="two numbers for each partition, once"):
                for k in range(2):
                    sp.dma_start(range_tab[k:k + 1, :].rearrange("o (p j) -> (o p) j", j=2),
                                 low_high[:, k, :]).then_inc(range_out, 16)
            sp.wait_ge(range_out, 32)
            sp.dma_start(base_all[:], range_tab[0:1, :].to_broadcast([128, STEPS])).then_inc(range_in, 16)
            sp.dma_start(base_f[:], range_tab[0:1, :]).then_inc(range_in, 16)
            sp.dma_start(high_f[:], range_tab[1:2, :]).then_inc(range_in, 16)

            def enc_store(c, s):
                sp.wait_ge(enc_staged, done(c))
                settle(sp)
                sp.dma_start(chunk_rows(p_tab[0], c), stage[s][:, 0]).then_inc(stored[s], 16)
                sp.dma_start(chunk_rows(q_tab[0][0:NPAD, :], c), stage[s][:, 1]).then_inc(stored[s], 16)

            with sp.Fori(0, ENC_SLOT - 1) as i:
                for s in range(2):
                    sp.wait_ge(enc_ps, done(i * 2 + s))
                    settle(sp)
                    sp.dma_start(x_t[s][:], io["x_t"][bass.ds(i * 2 + s + 2, 1)].rearrange("o f n -> (o f) n")).then_inc(xt_in[s], 16)
                    enc_store(i * 2 + s, s)
            sp.wait_ge(setup, 1)
            sp.dma_start(gate_w[HID:128, :, 0:2 * HID], io["whh"][:, :, 0:2 * HID]).then_inc(weights_in, 16)
            sp.dma_start(gate_w[HID:128, :, 3 * HID:4 * HID], io["whh"][:, :, 2 * HID:3 * HID]).then_inc(weights_in, 16)
            sp.dma_start(bias_zr[:], io["bih"][0:128, :]).then_inc(weights_in, 16)
            sp.dma_start(bias_hzr[:], io["bhh"][0:128, :]).then_inc(weights_in, 16)
            sp.dma_start(bias_in[:], io["bih"][128:192, :]).then_inc(weights_in, 16)
            sp.dma_start(bias_hn[HID:128, :], io["bhh"][128:192, :]).then_inc(weights_in, 16)
            sp.dma_start(ro_w1[HID:128, :], io["ro_W1"]).then_inc(weights_in, 16)
            sp.dma_start(ro_b1[:], io["ro_b1"]).then_inc(weights_in, 16)
            sp.dma_start(ro_w2b[:], io["ro_w2b"]).then_inc(weights_in, 16)
            for s in range(2):
                sp.dma_start(source[WINDOW:KEDGE, :, s, :], io["w1_edge"]).then_inc(weights_in, 16)
            sp.wait_ge(cleared, 1)
            for l in range(LAYERS):
                sp.dma_start(q_tab[l][NPAD:NWIN, :], zeros[0:WINDOW, 0:HID]).then_inc(zero_rows, 16)
            for c in (CHUNKS - 2, CHUNKS - 1):
                enc_store(c, c % 2)
            passes, slow = load_flags(sp)

            def lead(l, m, k, s):
                sp.wait_ge(added, slot_free(k, GATHER_SLOTS))
                settle(sp)
                sp.dma_start(idx[s][:], io["src"][bass.ds(m, 1)].rearrange("o p g -> (o p) g")).then_inc(idx_in[s], 16)

            def front(l, m, k, s):
                s = s % 2
                sp.wait_ge(combined, slot_free(k))
                settle(sp)
                sp.dma_start(pick[s][WINDOW:FEATS, :], io["edge_t"][bass.ds(m, 1)].rearrange("o d e -> (o d) e")).then_inc(edge_in[s], 16)
                base = sp.value_load(base_i[0:1, bass.ds(m, 1)], min_val=0, max_val=NODES)
                sp.dma_start(source[0:WINDOW, l, s, :], q_tab[l][bass.ds(base, WINDOW), :]).then_inc(edge_in[s], 16)

            def end_pass(l, w, k):
                sp.sem_inc(pass_read, 1)
                sp.wait_ge(windows, (passes + 1) * l + w + 2)
                settle(sp)

            def end_passes(l):
                sp.wait_ge(windows, (passes + 1) * (l + 1) + 1)
                settle(sp)

            def chunk_stage(l, j, c, s, last):
                if l == LAYERS - 1 and j == 2:
                    sp.wait_ge(norm, c * NORM_OPS + 1)
                    settle(sp)
                    sp.dma_start(x_rows[:], chunk_rows(io["x_pad"], c)).then_inc(xr_in, 16)

            sp.wait_ge(zero_rows, 16 * LAYERS)
            for l in range(LAYERS):
                all_stored(sp, l)
                run_layer(sp, l, passes, slow, lead, front, None, chunk_stage, end_pass, end_passes)

        @block.gpsimd
        def _(pool):
            nc.gpsimd.memset(ident[:], 1.0).then_inc(consts, 1)
            nc.gpsimd.iota(iota_i[:], pattern=[[1, WINDOW]], base=0, channel_multiplier=0)
            nc.gpsimd.iota(stair_i[:], pattern=[[CHUNK, LOOPS], [0, LOOP_STEPS]], base=0, channel_multiplier=0)
            nc.gpsimd.iota(rungs_i[:], pattern=[[WINDOW, MAX_PASSES]], base=0, channel_multiplier=0)
            pool.wait_ge(consts, 1)
            nc.gpsimd.affine_select(out=ident[:], in_=ident[:], compare_op=ALU.is_equal, fill=0.0, base=0,
                                    pattern=[[-1, 128]], channel_multiplier=1).then_inc(consts, 1)
            passes, slow = load_flags(pool)

            def lead(l, m, k, s):
                pool.wait_ge(idx_in[s], arrivals(k, s, 16, GATHER_SLOTS))
                pool.wait_ge(added, slot_free(k, GATHER_SLOTS))
                settle(pool)
                for g in range(EDGE_TILES):
                    pool.indirect_dma_start(
                        out=p_src[s][:, g, :], out_offset=None, in_=p_tab[l],
                        in_offset=bass.IndirectOffsetOnAxis(ap=idx[s][:, g:g + 1], axis=0)).then_inc(gathered[s], 16)

            for l in range(LAYERS):
                all_stored(pool, l)
                run_layer(pool, l, passes, slow, lead)

        @block.tensor
        def _(pe):
            pe.sem_inc(enc_ps, CREDIT)
            pe.sem_inc(enc_projected, CREDIT)
            pe.sem_inc(flipped, CREDIT)
            pe.sem_inc(combined, CREDIT)
            pe.sem_inc(scattered, CREDIT)

            def enc_hidden(c, s, n_in):
                pe.wait_ge(xt_in[s], n_in)
                pe.wait_ge(enc_h, slot_free(c))
                settle(pe)
                nc.tensor.matmul(enc_h_ps[s][HID:128, 0:CHUNK], enc_w[:], x_t[s][:], start=True, stop=True).then_inc(enc_ps, 1)

            def enc_project(c, s):
                pe.wait_ge(enc_h, done(c))
                pe.wait_ge(enc_staged, slot_free(c))
                hn = h_enc[s][:].rearrange("q (p j) -> q j p", j=4)
                for j in range(4):
                    last = nc.tensor.matmul(enc_pq_ps[s][0:CPART, j * 128:(j + 1) * 128], hn[HID:128, j, :],
                                            w1_nodes[HID:128, 0, :], start=True, stop=True)
                last.then_inc(enc_projected, 1)

            pe.wait_ge(enc_in, 48)
            for c in range(2):
                enc_hidden(c, c, 16)
            with pe.Fori(0, ENC_SLOT - 1) as i:
                for s in range(2):
                    enc_project(i * 2 + s, s)
                    enc_hidden(i * 2 + s + 2, s, i * 16 + 32)
            for c in (CHUNKS - 2, CHUNKS - 1):
                enc_project(c, c % 2)
            pe.wait_ge(weights_in, 16 * 13)
            for l in range(LAYERS):
                pe.wait_ge(enc_h, done(CHUNKS - 1))
                if l:
                    pe.wait_ge(vw_sb, l)
                nc.tensor.matmul(zr_ps[0:HID + 1, 0:3 * HID], w2t_b2[:, l, :], wih[:, l, :], start=True, stop=True).then_inc(vw_ps, 1)
            pe.wait_ge(vw_sb, LAYERS)
            pe.wait_ge(cleared, 1)
            pe.wait_ge(consts, 2)
            pe.wait_ge(enc_staged, done(CHUNKS - 1))
            passes, slow = load_flags(pe)

            def lead(l, m, k, s):
                s = s % 2
                pe.wait_ge(hot_t_ready, done(k))
                pe.wait_ge(pick_ready, single_free(k))
                for g in range(EDGE_TILES):
                    last = nc.tensor.transpose(hott_ps[0:WINDOW, g * 128:(g + 1) * 128], hot_t[s][:, g, :], ident[:])
                last.then_inc(flipped, 1)

            def front(l, m, k, s):
                s = s % 2
                pe.wait_ge(pick_ready, done(k))
                pe.wait_ge(edge_in[s], arrivals(k, s, 32))
                pe.wait_ge(added, slot_free(k))
                for g in range(EDGE_TILES):
                    last = nc.tensor.matmul(pre_ps[s][:, g, :], pick[s][0:KEDGE, g * 128:(g + 1) * 128],
                                            source[0:KEDGE, l, s, :], start=True, stop=True)
                last.then_inc(combined, 1)

            def back(l, m, k, s):
                s = s % 2
                pe.wait_ge(hot_ready, done(k))
                pe.wait_ge(msg_ready, done(k))
                pe.wait_ge(summed, single_free(k))
                for g in range(EDGE_TILES):
                    last = nc.tensor.matmul(sum_ps[0:HID + 1, 0:WINDOW], msg[s][:, g, :], hot[s][:, g, :],
                                            start=(g == 0), stop=(g == EDGE_TILES - 1))
                last.then_inc(scattered, 1)

            def chunk_stage(l, j, c, s, last):
                n = before(l, c)
                if j == 0:
                    pe.wait_ge(chunk_in, n + 1)
                    if l == LAYERS - 1:
                        pe.wait_ge(hid_ready, c + 1)
                    for ps, g in ((zr_ps, 0), (n_ps, 2 * HID)):
                        nc.tensor.matmul(ps[:, 0:CHUNK], gate_w[:, l, g:g + 128], chunk[:], start=True, stop=False)
                        end = nc.tensor.matmul(ps[:, 0:CHUNK], deg_w[HID:HID + 1, l, g:g + 128],
                                               chunk_deg[HID:HID + 1, :], start=False, stop=True)
                    end.then_inc(gates_ps, 1)
                if j == 3:
                    pe.wait_ge(gru, GRU_OPS * (n + 1) + 1)
                    if l < LAYERS - 1:
                        pe.wait_ge(staged, n + 1)
                        hn = h_next[:].rearrange("q (p j) -> q j p", j=4)
                        for q in range(4):
                            end = nc.tensor.matmul(pq_ps[0:CPART, q * 128:(q + 1) * 128], hn[HID:128, q, :],
                                                   w1_nodes[HID:128, l + 1, :], start=True, stop=True)
                        end.then_inc(projected, 1)
                    else:
                        settle(pe)
                        nc.tensor.matmul(zr_ps[0:HID, 0:CHUNK], ro_w1[HID:128, :], h_next[HID:128, :],
                                         start=True, stop=True).then_inc(hid_ps, 1)
                if j == 4 and l == LAYERS - 1:
                    pe.wait_ge(hid_ready, c + 2)
                    pe.wait_ge(norm, c * NORM_OPS + 1)
                    hv = hid[:].rearrange("q (p j) -> q j p", j=4)
                    for q in range(4):
                        end = nc.tensor.matmul(pq_ps[0:CPART, q * HID:(q + 1) * HID], hv[:, q, :], ro_w2b[:],
                                               start=True, stop=True)
                    end.then_inc(y_ps, 1)

            for l in range(LAYERS):
                if l == LAYERS - 1:
                    pe.wait_ge(staged, CHUNKS * l + 1)
                run_layer(pe, l, passes, slow, lead, front, back, chunk_stage)

        @block.scalar
        def _(act):
            act.sem_inc(enc_h, CREDIT)
            act.wait_ge(enc_in, 48)

            def enc_hidden(c, s):
                act.wait_ge(enc_ps, done(c))
                act.wait_ge(enc_kept, slot_free(c))
                act.wait_ge(enc_projected, slot_free(c))
                nc.scalar.activation(h_enc[s][HID:128, :], enc_h_ps[s][HID:128, 0:CHUNK], ACT.Identity,
                                     bias=enc_b[HID:128, :]).then_inc(enc_h, 1)

            with act.Fori(0, ENC_SLOT) as i:
                for s in range(2):
                    enc_hidden(i * 2 + s, s)
            act.wait_ge(setup, 1)
            for l in range(LAYERS):
                act.wait_ge(vw_ps, l + 1)
                nc.scalar.copy(gate_w[0:HID, l, 0:3 * HID], zr_ps[0:HID, 0:3 * HID])
                nc.scalar.copy(deg_w[HID:HID + 1, l, 0:3 * HID], zr_ps[HID:HID + 1, 0:3 * HID]).then_inc(vw_sb, 1)
            passes, slow = load_flags(act)
            act.wait_ge(cleared, 1)
            act.wait_ge(bias_ready, 1)
            for credit in (pick_ready, msg_ready):
                act.sem_inc(credit, CREDIT)
            for credit in (staged, h_kept, hid_ready):
                act.sem_inc(credit, 1)
            act.wait_ge(enc_kept, done(CHUNKS - 1))

            def lead(l, m, k, s):
                s = s % 2
                act.wait_ge(flipped, done(k))
                act.wait_ge(combined, slot_free(k))
                nc.scalar.copy(pick[s][0:WINDOW, :], hott_ps[0:WINDOW, :]).then_inc(pick_ready, 1)

            def back(l, m, k, s):
                s = s % 2
                act.wait_ge(added, done(k))
                act.wait_ge(scattered, slot_free(k))
                nc.scalar.activation(msg[s][:, :, 0:HID], pre[s][:], ACT.Relu).then_inc(msg_ready, 1)

            def chunk_stage(l, j, c, s, last):
                n = before(l, c)
                if j == 0:
                    act.wait_ge(summed, done(last))
                    act.wait_ge(gru, GRU_OPS * n + 1)
                    if l:
                        act.wait_ge(h_kept, CHUNKS * l + 1)
                    nc.scalar.copy(chunk[:], state[:, cols(c)])
                    nc.scalar.copy(chunk_deg[HID:HID + 1, :], degree[HID:HID + 1, cols(c)]).then_inc(chunk_in, 1)
                if j == 1:
                    act.wait_ge(gates_ps, n + 1)
                    nc.scalar.activation(zr[:], zr_ps[:, 0:CHUNK], ACT.Sigmoid, bias=bias_zr[:, l:l + 1]).then_inc(zr_ready, 1)
                if j == 2:
                    act.wait_ge(gru, GRU_OPS * n + 4)
                    nc.scalar.activation(n_hi[HID:128, :], npre[:], ACT.Tanh, bias=bias_in[:, l:l + 1]).then_inc(n_ready, 1)
                if j == 3 and l < LAYERS - 1:
                    act.wait_ge(gru, GRU_OPS * (n + 1) + 1)
                    nc.scalar.copy(state[HID:128, cols(c)], h_next[HID:128, :]).then_inc(h_kept, 1)
                if j == 4 and l < LAYERS - 1:
                    act.wait_ge(projected, n + 1)
                    act.wait_ge(stored[s], stored_before(l, c, s))
                    nc.scalar.copy(stage[s][:].rearrange("p t j f -> p j t f"), pq_view(pq_ps)).then_inc(staged, 1)
                    act.wait_ge(staged, n + 2)
                    act.dma_start(chunk_rows(p_tab[l + 1], c), stage[s][:, 0]).then_inc(stored[s], 16)
                    act.dma_start(chunk_rows(q_tab[l + 1][0:NPAD, :], c), stage[s][:, 1]).then_inc(stored[s], 16)
                if j == 4 and l == LAYERS - 1:
                    act.wait_ge(hid_ps, c + 1)
                    act.wait_ge(norm, c * NORM_OPS + 1)
                    nc.scalar.activation(hid[0:HID, :], zr_ps[0:HID, 0:CHUNK], ACT.Relu, bias=ro_b1[:]).then_inc(hid_ready, 1)
                if j == 6 and l == LAYERS - 1:
                    act.wait_ge(norm, c * NORM_OPS + 8)
                    nc.scalar.activation(sd[:], veps[:], ACT.Sqrt).then_inc(sd_ready, 1)
                if j == 7 and l == LAYERS - 1:
                    act.wait_ge(norm, (c + 1) * NORM_OPS + 1)
                    if isinstance(c, int) and c == CHUNKS - 1:
                        act.dma_start(io["out"][c * CHUNK:NODES, :].rearrange("(p j) f -> p j f", j=4),
                                      y_out[0:LAST_PART]).then_inc(out_done, 16)
                    else:
                        act.dma_start(chunk_rows(io["out"][0:(CHUNKS - 1) * CHUNK, :], c), y_out[:]).then_inc(out_done, 16)

            for l in range(LAYERS):
                run_layer(act, l, passes, slow, lead, None, back, chunk_stage)
            act.wait_ge(out_done, 16 * CHUNKS)

        @block.vector
        def _(dve):
            for credit in (enc_kept, enc_staged, hot_t_ready, hot_ready, added, summed):
                dve.sem_inc(credit, CREDIT)
            dve.sem_inc(gru, 1)
            dve.sem_inc(norm, 1)
            nc.vector.memset(gate_w[:], 0.0)
            nc.vector.memset(deg_w[:], 0.0).then_inc(setup, 1)
            dve.wait_ge(steps_in, 16)
            nc.vector.tensor_reduce(low_high[:, 0, :], dst_steps, AX.X, ALU.min)
            nc.vector.tensor_reduce(low_high[:, 1, :], dst_steps, AX.X, ALU.max).then_inc(reduced, 1)
            dve.wait_ge(reduced, 1)
            nc.vector.memset(zeros[:], 0.0)
            nc.vector.memset(state[0:HID, :], 0.0)
            nc.vector.memset(state[HID:128, NPAD:NWIN], 0.0)
            nc.vector.memset(degree[HID:HID + 1, :], 0.0)
            nc.vector.memset(hid[HID:HID + 1, :], 1.0)
            for s in range(2):
                nc.vector.memset(pick[s][WINDOW:128, :], 1.0)
                last = nc.vector.memset(msg[s][:], 1.0)
            last.then_inc(cleared, 1)

            def enc_chunk(c, s, n_stored):
                dve.wait_ge(enc_h, done(c))
                nc.vector.tensor_copy(state[HID:128, cols(c)], h_enc[s][HID:128, :]).then_inc(enc_kept, 1)
                dve.wait_ge(enc_projected, done(c))
                if n_stored is not None:
                    dve.wait_ge(stored[s], n_stored)
                nc.vector.tensor_copy(stage[s][:].rearrange("p t j f -> p j t f"), pq_view(enc_pq_ps[s])).then_inc(enc_staged, 1)

            for c in range(2):
                enc_chunk(c, c, None)

            chain = [1]

            def link(op):
                chain[0] += 1
                op.then_inc(setup, 1)
                dve.wait_ge(setup, chain[0])

            dve.wait_ge(consts, 2)
            nc.vector.tensor_copy(iota_ps, iota_i[:])
            nc.vector.tensor_copy(stair[:], stair_i[:])
            link(nc.vector.tensor_copy(rungs[:], rungs_i[:]))
            dve.wait_ge(dst_in, 16)
            dve.wait_ge(range_in, 48)
            nc.vector.tensor_tensor(rel[:], dst_i[:], base_all[:].unsqueeze(2).to_broadcast([128, STEPS, EDGE_TILES]), ALU.subtract)
            nc.vector.tensor_copy(start_f[:], base_f[:])
            nc.vector.tensor_scalar(base_i[:], base_f[:], float(NODES), None, ALU.min)
            nc.vector.tensor_tensor(late[:], base_f[:], stair[:], ALU.is_lt)
            link(nc.vector.tensor_tensor(spread[:], high_f[:], base_f[:], ALU.subtract))
            nc.vector.tensor_reduce(late_n[:], late[:], AX.X, ALU.add)
            link(nc.vector.tensor_reduce(widest[:], spread[:], AX.X, ALU.max))
            link(nc.vector.tensor_scalar(reach[:], rungs[:], widest[0:1, 0:1], None, ALU.is_le))
            link(nc.vector.tensor_reduce(passes_f[:], reach[:], AX.X, ALU.add))
            link(nc.vector.scalar_tensor_tensor(slow_f[:], passes_f[:], -1.0, late_n[:], ALU.add, ALU.add))
            nc.vector.tensor_copy(flags[0:1, 0:1], passes_f[:])
            nc.vector.tensor_copy(flags[0:1, 1:2], slow_f[:]).then_inc(windows, 1)

            with dve.Fori(1, ENC_SLOT) as i:
                for s in range(2):
                    enc_chunk(i * 2 + s, s, i * 32)
            dve.wait_ge(weights_in, 16 * 13)
            nc.vector.tensor_tensor(bias_zr[:], bias_zr[:], bias_hzr[:], ALU.add).then_inc(bias_ready, 1)
            dve.wait_ge(cleared, 1)
            passes, slow = load_flags(dve)

            def rel_of(m):
                return rel[:, bass.ds(m, 1), :].rearrange("p o g -> p (o g)").unsqueeze(2).to_broadcast([128, EDGE_TILES, WINDOW])

            node = iota_ps.unsqueeze(1).to_broadcast([128, EDGE_TILES, WINDOW])

            def lead(l, m, k, s):
                s = s % 2
                dve.wait_ge(flipped, slot_free(k))
                nc.vector.tensor_tensor(hot_t[s][:], rel_of(m), node, ALU.is_equal).then_inc(hot_t_ready, 1)

            def front(l, m, k, s):
                s = s % 2
                dve.wait_ge(scattered, slot_free(k))
                nc.vector.tensor_tensor(hot[s][:], rel_of(m), node, ALU.is_equal).then_inc(hot_ready, 1)

            def back(l, m, k, s):
                r, s = s, s % 2
                dve.wait_ge(gathered[r], arrivals(k, r, 16 * EDGE_TILES, GATHER_SLOTS))
                dve.wait_ge(combined, done(k))
                dve.wait_ge(msg_ready, slot_free(k))
                nc.vector.tensor_tensor(pre[s][:], pre_ps[s][:], p_src[r][:], ALU.add).then_inc(added, 1)
                base = dve.value_load(base_i[0:1, bass.ds(m, 1)], min_val=0, max_val=NODES)
                dve.wait_ge(scattered, done(k))
                dve.wait_ge(summed, single_free(k))
                here = bass.ds(base, WINDOW)
                nc.vector.tensor_tensor(state[0:HID, here], sum_ps[0:HID, 0:WINDOW], state[0:HID, here], ALU.add)
                nc.vector.tensor_tensor(degree[HID:HID + 1, here], sum_ps[HID:HID + 1, 0:WINDOW],
                                        degree[HID:HID + 1, here], ALU.add).then_inc(summed, 1)

            def end_pass(l, w, k):
                dve.wait_ge(hot_ready, done(k))
                dve.wait_ge(pass_read, passes * l + w + 1)
                nc.vector.tensor_scalar(rel[:], rel[:], float(-WINDOW), None, ALU.add)
                nc.vector.tensor_scalar(start_f[:], start_f[:], float(WINDOW), None, ALU.add).then_inc(window_step, 1)
                dve.wait_ge(window_step, (passes + 1) * l + w + 1)
                nc.vector.tensor_scalar(base_i[:], start_f[:], float(NODES), None, ALU.min).then_inc(windows, 1)
                dve.wait_ge(windows, (passes + 1) * l + w + 2)
                settle(dve)

            def end_passes(l):
                nc.vector.tensor_tensor(rel[:], dst_i[:], base_all[:].unsqueeze(2).to_broadcast([128, STEPS, EDGE_TILES]), ALU.subtract)
                nc.vector.tensor_copy(start_f[:], base_f[:]).then_inc(window_step, 1)
                nc.vector.tensor_scalar(base_i[:], base_f[:], float(NODES), None, ALU.min).then_inc(windows, 1)
                dve.wait_ge(windows, (passes + 1) * (l + 1) + 1)
                settle(dve)

            def chunk_stage(l, j, c, s, last):
                n = before(l, c)
                g0 = GRU_OPS * n + 1
                if j == 1:
                    dve.wait_ge(chunk_in, n + 1)
                    dve.wait_ge(summed, done(last))
                    nc.vector.tensor_copy(state[0:HID, cols(c)], zeros[0:HID, :])
                    nc.vector.tensor_copy(degree[HID:HID + 1, cols(c)], zeros[HID:HID + 1, :]).then_inc(gru, 1)
                    dve.wait_ge(zr_ready, n + 1)
                    nc.vector.scalar_tensor_tensor(rn[:], n_ps[HID:128, 0:CHUNK], bias_hn[HID:128, l:l + 1], zr[HID:128, :],
                                                   ALU.add, ALU.mult).then_inc(gru, 1)
                    dve.wait_ge(gru, g0 + 2)
                    nc.vector.tensor_tensor(npre[:], n_ps[0:HID, 0:CHUNK], rn[:], ALU.add).then_inc(gru, 1)
                if j == 2:
                    dve.wait_ge(n_ready, n + 1)
                    nc.vector.tensor_tensor(diff[:], chunk[HID:128, :], n_hi[HID:128, :], ALU.subtract).then_inc(gru, 1)
                    dve.wait_ge(gru, g0 + 4)
                    nc.vector.tensor_tensor(zdiff[HID:128, :], zr[0:HID, :], diff[:], ALU.mult).then_inc(gru, 1)
                    dve.wait_ge(gru, g0 + 5)
                    if l < LAYERS - 1:
                        if not (l == 0 and isinstance(c, int) and c == 0):
                            dve.wait_ge(staged, n + 1)
                            dve.wait_ge(h_kept, n + 1)
                    else:
                        dve.wait_ge(hid_ready, c + 1)
                    nc.vector.tensor_tensor(h_next[HID:128, :], n_hi[HID:128, :], zdiff[HID:128, :], ALU.add).then_inc(gru, 1)
                if j == 5 and l == LAYERS - 1:
                    n0 = c * NORM_OPS + 1
                    dve.wait_ge(y_ps, c + 1)
                    dve.wait_ge(xr_in, c * 16 + 16)
                    nc.vector.tensor_tensor(y[:], pq_ps[0:CPART, 0:4 * HID].rearrange("p (j f) -> p j f", j=4), x_rows[:], ALU.add).then_inc(norm, 1)
                    dve.wait_ge(norm, n0 + 1)
                    nc.vector.tensor_reduce(ysum[:], y[:], AX.X, ALU.add).then_inc(norm, 1)
                    dve.wait_ge(norm, n0 + 2)
                    nc.vector.tensor_scalar(ymean[:], ysum[:], 1.0 / HID, None, ALU.mult).then_inc(norm, 1)
                    dve.wait_ge(norm, n0 + 3)
                    nc.vector.tensor_tensor(yc[:], y[:], ymean[:].unsqueeze(2).to_broadcast([CPART, 4, HID]), ALU.subtract).then_inc(norm, 1)
                    dve.wait_ge(norm, n0 + 4)
                    nc.vector.tensor_tensor(ysq[:], yc[:], yc[:], ALU.mult).then_inc(norm, 1)
                    dve.wait_ge(norm, n0 + 5)
                    nc.vector.tensor_reduce(vsum[:], ysq[:], AX.X, ALU.add).then_inc(norm, 1)
                    dve.wait_ge(norm, n0 + 6)
                    nc.vector.tensor_scalar(veps[:], vsum[:], 1.0 / HID, EPS, ALU.mult, ALU.add).then_inc(norm, 1)
                if j == 6 and l == LAYERS - 1:
                    n0 = c * NORM_OPS + 1
                    dve.wait_ge(sd_ready, c + 1)
                    nc.vector.reciprocal(rstd[:], sd[:]).then_inc(norm, 1)
                    dve.wait_ge(norm, n0 + 8)
                    if isinstance(c, int) and c == 0:
                        pass
                    else:
                        dve.wait_ge(out_done, c * 16)
                    nc.vector.tensor_tensor(y_out[:], yc[:], rstd[:].unsqueeze(2).to_broadcast([CPART, 4, HID]), ALU.mult).then_inc(norm, 1)

            for l in range(LAYERS):
                if l:
                    dve.wait_ge(gru, GRU_OPS * CHUNKS * l + 1)
                run_layer(dve, l, passes, slow, lead, front, back, chunk_stage, end_pass, end_passes)


def kernel(**inputs):
    import numpy as np
    import concourse.bacc as bacc
    from concourse.bass_utils import run_bass_kernel_spmd

    a = {k.replace("L0_gnn_", ""): np.asarray(v) for k, v in inputs.items()}
    padded = STEPS * STEP

    def pad(v, n, fill=0):
        out = np.full((n,) + v.shape[1:], fill, v.dtype)
        out[:len(v)] = v
        return out

    src = pad(a["src"], padded).reshape(STEPS, EDGE_TILES, 128)
    dst = pad(a["dst"], padded, NODES)
    edge = pad(a["edge_attr_16"], padded)
    x = pad(a["x"], NPAD)

    def gates(v):
        return v.reshape(v.shape[:-1] + (3, HID))[..., [1, 0, 2], :].reshape(v.shape)

    w1 = a["msg_W1"]
    arrays = {
        "x_t": x.reshape(CHUNKS, CHUNK, HID).transpose(0, 2, 1),
        "x_pad": x,
        "src": src.transpose(0, 2, 1),
        "dst": dst.reshape(STEPS, EDGE_TILES, 128).transpose(2, 0, 1),
        "dst_steps": dst.reshape(STEPS // 2, 2, STEP),
        "edge_t": edge.reshape(STEPS, STEP, EDGE_DIM).transpose(0, 2, 1),
        "enc_W": a["enc_W"],
        "enc_b": a["enc_b"][:, None],
        "w1_nodes": np.concatenate([w1[:, :HID], w1[:, HID:2 * HID]], 2).transpose(1, 0, 2),
        "w1_edge": np.concatenate([w1[:, 2 * HID:], a["msg_b1"][:, None]], 1).transpose(1, 0, 2),
        "w2t_b2": np.concatenate([a["msg_W2"], a["msg_b2"][:, None]], 1).transpose(2, 0, 1),
        "wih": gates(a["gru_Wih"]).transpose(1, 0, 2),
        "whh": gates(a["gru_Whh"]).transpose(1, 0, 2),
        "bih": gates(a["gru_bih"]).T,
        "bhh": gates(a["gru_bhh"]).T,
        "ro_W1": a["ro_W1"],
        "ro_b1": a["ro_b1"][:, None],
        "ro_w2b": np.concatenate([a["ro_W2"], a["ro_b2"][None]], 0),
    }
    nc = bacc.Bacc("TRN2", target_bir_lowering=False, num_devices=1)
    io = {}
    for name, v in arrays.items():
        arrays[name] = v = np.ascontiguousarray(v)
        dt = U32 if name == "src" else I32 if name.startswith("dst") else F32
        if name == "src":
            arrays[name] = v = v.view(np.uint32)
        io[name] = nc.dram_tensor(f"in_{name}", v.shape, dt, kind="ExternalInput").ap()
    io["out"] = nc.dram_tensor("out", (NODES, HID), F32, kind="ExternalOutput").ap()
    build(nc, io)
    result = run_bass_kernel_spmd(nc, [{f"in_{k}": v for k, v in arrays.items()}], core_ids=[0])
    return result.results[0]["out"]
```

```python
import concourse.bass as bass
from concourse import mybir
from contextlib import ExitStack

F32 = mybir.dt.float32
BF16 = mybir.dt.bfloat16
I32 = mybir.dt.int32
U32 = mybir.dt.uint32
ALU = mybir.AluOpType
ACT = mybir.ActivationFunctionType
AX = mybir.AxisListType

LAYERS = 3
HID = 64
EDGE_DIM = 16
NODES = 12500
EDGES = 212500
EDGE_TILES = 8
STEP = EDGE_TILES * 128
STEPS = -(-EDGES // STEP)
WINDOW = 96
FEATS = WINDOW + EDGE_DIM
KEDGE = FEATS + 1
LOOP_STEPS = 8
LOOPS = STEPS // LOOP_STEPS
CHUNK = 448
CPART = CHUNK // 4
CHUNKS = -(-NODES // CHUNK)
LOOPED = LOOPS - 1
NPAD = CHUNKS * CHUNK
NWIN = NPAD + WINDOW
MAX_PASSES = NODES // WINDOW + 1
LAST_PART = (NODES - (CHUNKS - 1) * CHUNK) // 4
GATHER_SLOTS = 4
CREDIT = GATHER_SLOTS
ENC_SLOT = CHUNKS // 2
TAIL = [(0, 0), (1, 0), (0, 1), (0, 2), (0, 3), (2, 0), (1, 1), (0, 4), (1, 2), (0, 5), (1, 3), (0, 6),
        (2, 1), (1, 4), (0, 7), (2, 2), (1, 5), (2, 3), (1, 6), (2, 4), (1, 7), (2, 5), (2, 6), (2, 7)]
assert CHUNKS - LOOPED == 3
GRU_OPS = 6
NORM_OPS = 9
EPS = 1e-5


def build(nc, io):
    with ExitStack() as ctx:
        def sb(name, shape, dt=F32):
            return ctx.enter_context(nc.sbuf_tensor(name, shape, dt))

        def sem(name):
            return ctx.enter_context(nc.semaphore(name))

        p_tab = [nc.dram_tensor(f"p_tab{l}", [NPAD, HID], F32).ap() for l in range(LAYERS)]
        q_tab = [nc.dram_tensor(f"q_tab{l}", [NWIN, HID], F32).ap() for l in range(LAYERS)]
        range_tab = nc.dram_tensor("range_tab", [2, STEPS], F32).ap()

        ident = sb("ident", [128, 128], BF16)
        zeros = sb("zeros", [128, CHUNK])
        iota_i = sb("iota_i", [128, WINDOW], I32)
        stair_i = sb("stair_i", [1, STEPS], I32)
        stair = sb("stair", [1, STEPS])
        rungs_i = sb("rungs_i", [1, MAX_PASSES], I32)
        rungs = sb("rungs", [1, MAX_PASSES])
        enc_w = sb("enc_w", [HID, HID])
        enc_b = sb("enc_b", [128, 1])
        w1_nodes = sb("w1_nodes", [128, LAYERS, 2 * HID])
        w2t_b2 = sb("w2t_b2", [HID, LAYERS, HID + 1])
        wih = sb("wih", [HID, LAYERS, 3 * HID])
        gate_w = sb("gate_w", [128, LAYERS, 4 * HID])
        deg_w = sb("deg_w", [128, LAYERS, 4 * HID])
        bias_zr = sb("bias_zr", [128, LAYERS])
        bias_hzr = sb("bias_hzr", [128, LAYERS])
        bias_in = sb("bias_in", [HID, LAYERS])
        bias_hn = sb("bias_hn", [128, LAYERS])
        ro_w1 = sb("ro_w1", [128, HID])
        ro_b1 = sb("ro_b1", [HID, 1])
        ro_w2b = sb("ro_w2b", [HID + 1, HID])
        low_high = sb("low_high", [STEPS // 2, 2, 2])
        dst_i = sb("dst_i", [128, STEPS, EDGE_TILES], I32)
        base_all = sb("base_all", [128, STEPS])
        rel = sb("rel", [128, STEPS, EDGE_TILES])
        base_f = sb("base_f", [1, STEPS])
        high_f = sb("high_f", [1, STEPS])
        spread = sb("spread", [1, STEPS])
        late = sb("late", [1, STEPS])
        start_f = sb("start_f", [1, STEPS])
        base_i = sb("base_i", [1, STEPS], I32)
        widest = sb("widest", [1, 1])
        reach = sb("reach", [1, MAX_PASSES])
        passes_f = sb("passes_f", [1, 1])
        late_n = sb("late_n", [1, 1])
        slow_f = sb("slow_f", [1, 1])
        flags = sb("flags", [1, 2], I32)
        state = sb("state", [128, NWIN])
        degree = sb("degree", [128, NWIN])
        dst_steps = degree[0:STEPS // 2, 0:2 * STEP].bitcast(I32).rearrange("p (j e) -> p j e", j=2)
        idx = [sb(f"idx{s}", [128, EDGE_TILES], U32) for s in range(GATHER_SLOTS)]
        p_src = [sb(f"p_src{s}", [128, EDGE_TILES, HID]) for s in range(GATHER_SLOTS)]
        hot_t = [sb(f"hot_t{s}", [128, EDGE_TILES, WINDOW], BF16) for s in range(2)]
        hot = [sb(f"hot{s}", [128, EDGE_TILES, WINDOW]) for s in range(2)]
        pick = [sb(f"pick{s}", [128, STEP]) for s in range(2)]
        source = sb("source", [128, LAYERS, 2, HID])
        pre = [sb(f"pre{s}", [128, EDGE_TILES, HID]) for s in range(2)]
        msg = [sb(f"msg{s}", [128, EDGE_TILES, HID + 1]) for s in range(2)]
        x_t = [sb(f"x_t{s}", [HID, CHUNK]) for s in range(2)]
        chunk = [sb(f"chunk{s}", [128, CHUNK]) for s in range(2)]
        h_enc = chunk
        chunk_deg = [sb(f"chunk_deg{s}", [128, CHUNK]) for s in range(2)]
        zr = [sb(f"zr{s}", [128, CHUNK]) for s in range(2)]
        rn = sb("rn", [HID, CHUNK])
        npre = sb("npre", [HID, CHUNK])
        n_hi = sb("n_hi", [128, CHUNK])
        diff = sb("diff", [HID, CHUNK])
        zdiff = sb("zdiff", [128, CHUNK])
        h_next = sb("h_next", [128, CHUNK])
        stage = [sb(f"stage{s}", [CPART, 2, 4, HID]) for s in range(2)]
        hid = sb("hid", [HID + 1, CHUNK])
        x_rows = sb("x_rows", [CPART, 4, HID])
        y = sb("y", [CPART, 4, HID])
        yc = sb("yc", [CPART, 4, HID])
        ysq = sb("ysq", [CPART, 4, HID])
        ysum = sb("ysum", [CPART, 4])
        ymean = sb("ymean", [CPART, 4])
        vsum = sb("vsum", [CPART, 4])
        veps = sb("veps", [CPART, 4])
        sd = sb("sd", [CPART, 4])
        rstd = sb("rstd", [CPART, 4])
        y_out = sb("y_out", [CPART, 4, HID])

        bank = [ctx.enter_context(nc.psum_tensor(f"bank{i}", [128, 512], F32)) for i in range(5)]
        iota_ps = bank[0][:, 0:WINDOW]
        sum_ps = bank[1]
        zr_ps, n_ps, pq_ps = bank[2], bank[3], bank[4]
        hott_ps = ctx.enter_context(nc.psum_tensor("hott_ps", [128, STEP], BF16))
        pre_ps = [ctx.enter_context(nc.psum_tensor(f"pre_ps{s}", [128, EDGE_TILES, HID], F32)) for s in range(2)]

        consts = sem("consts")
        dst_in = sem("dst_in")
        steps_in = sem("steps_in")
        weights_in = sem("weights_in")
        reduced = sem("reduced")
        range_out = sem("range_out")
        range_in = sem("range_in")
        setup = sem("setup")
        vw_ps = sem("vw_ps")
        vw_sb = sem("vw_sb")
        zero_rows = sem("zero_rows")
        cleared = sem("cleared")
        sums_clear = sem("sums_clear")
        bias_ready = sem("bias_ready")
        xt_in = [sem(f"xt_in{s}") for s in range(2)]
        enc_in = sem("enc_in")
        enc_ps = sem("enc_ps")
        enc_h = sem("enc_h")
        enc_kept = sem("enc_kept")
        enc_projected = sem("enc_projected")
        enc_staged = sem("enc_staged")
        stored = [sem(f"stored{s}") for s in range(2)]
        idx_in = [sem(f"idx_in{s}") for s in range(GATHER_SLOTS)]
        edge_in = [sem(f"edge_in{s}") for s in range(2)]
        pace = sem("pace")
        gathered = [sem(f"gathered{s}") for s in range(GATHER_SLOTS)]
        hot_t_ready = sem("hot_t_ready")
        hot_ready = sem("hot_ready")
        flipped = sem("flipped")
        pick_ready = sem("pick_ready")
        combined = sem("combined")
        added = sem("added")
        msg_ready = sem("msg_ready")
        scattered = sem("scattered")
        summed = sem("summed")
        windows = sem("windows")
        window_step = sem("window_step")
        pass_read = sem("pass_read")
        chunk_in = sem("chunk_in")
        gates_ps = sem("gates_ps")
        zr_ready = sem("zr_ready")
        gru = sem("gru")
        n_ready = sem("n_ready")
        h_kept = sem("h_kept")
        projected = sem("projected")
        staged = sem("staged")
        hid_ps = sem("hid_ps")
        hid_ready = sem("hid_ready")
        y_ps = sem("y_ps")
        xr_in = sem("xr_in")
        norm = sem("norm")
        sd_ready = sem("sd_ready")
        out_done = sem("out_done")

        def done(k):
            return k + (CREDIT + 1)

        def slot_free(k, slots=2):
            return k + (CREDIT + 1 - slots)

        def single_free(k):
            return k + CREDIT

        def arrivals(k, s, each, slots=2):
            return (k - s) * (each // slots) + each

        def cols(c):
            return bass.ds(c * CHUNK, CHUNK)

        def before(l, c):
            return c + l * CHUNKS

        gate_ps = [[zr_ps, n_ps], [ps[:].rearrange("p t f -> p (t f)") for ps in pre_ps]]

        def two_slots(c):
            return int(isinstance(c, int) and c >= LOOPED)

        def stored_before(l, c, s):
            if s == 0:
                return 32 * (min(c, LOOPED) + ENC_SLOT + (LOOPED + 1) * l if isinstance(c, int)
                             else c + (ENC_SLOT + (LOOPED + 1) * l))
            return 32 * (ENC_SLOT + 2 * l + (c - LOOPED) // 2)

        def all_stored(eng, l):
            eng.wait_ge(stored[0], 32 * (ENC_SLOT + (LOOPED + 1) * l))
            eng.wait_ge(stored[1], 32 * (ENC_SLOT + 2 * l))

        def settle(eng):
            eng.sem_inc(pace, 1)

        def load_flags(eng):
            eng.wait_ge(windows, 1)
            return (eng.value_load(flags[0:1, 0:1], min_val=1, max_val=MAX_PASSES),
                    eng.value_load(flags[0:1, 1:2], min_val=0, max_val=STEPS + MAX_PASSES))

        def run_layer(eng, l, passes, slow, lead=None, front=None, back=None, trail=None, chunk_stage=None, end_pass=None,
                      end_passes=None):
            k0 = 0 if l == 0 else passes * (l * STEPS)
            last = k0 + passes * STEPS - 1

            def part(what, i, k, g, j):
                if what:
                    n = i * LOOP_STEPS + j
                    what(l, n, k + n, g + n, j % GATHER_SLOTS)

            def round_of_steps(i, k, g, with_chunk, first=False, final=False):
                for j in range(LOOP_STEPS):
                    if j + 2 < LOOP_STEPS or not final:
                        part(lead, i, k, g, j + 2)
                    if j + 1 < LOOP_STEPS or not final:
                        part(front, i, k, g, j + 1)
                    if j or not first:
                        part(trail, i, k, g, j - 1)
                    part(back, i, k, g, j)
                    if with_chunk and chunk_stage:
                        chunk_stage(l, j, i - 1, 0, k + i * LOOP_STEPS - 1)

            def one_pass(k, g, with_chunks):
                part(lead, 0, k, g, 0)
                part(lead, 0, k, g, 1)
                part(front, 0, k, g, 0)
                round_of_steps(0, k, g, False, first=True)
                with eng.Fori(1, LOOPS - 1) as i:
                    round_of_steps(i, k, g, with_chunks)
                round_of_steps(LOOPS - 1, k, g, with_chunks, final=True)
                part(trail, LOOPS - 1, k, g, LOOP_STEPS - 1)

            with eng.If(slow == 0):
                one_pass(k0, l * STEPS, True)
            with eng.Else():
                with eng.Fori(0, passes) as w:
                    one_pass(k0 + w * STEPS, 0, False)
                    if end_pass:
                        end_pass(l, w, k0 + w * STEPS + (STEPS - 1))
                if end_passes:
                    end_passes(l)
                if chunk_stage:
                    with eng.Fori(0, LOOPED) as c:
                        for j in range(LOOP_STEPS):
                            chunk_stage(l, j, c, 0, last)
            if chunk_stage:
                for n, j in TAIL:
                    chunk_stage(l, j, LOOPED + n, (LOOPED + n) % 2, last)

        def chunk_rows(table, c):
            rows = table.rearrange("(c p j) f -> c p j f", p=CPART, j=4)
            return rows[bass.ds(c, 1)].rearrange("o p j f -> (o p) j f")

        enc_h_ps = [zr_ps, n_ps]
        enc_pq_ps = [pq_ps, sum_ps]

        def pq_view(ps):
            return ps[0:CPART, :].rearrange("p (j t f) -> p j t f", j=4, t=2)

        block = ctx.enter_context(nc.Block())

        @block.sync
        def _(sp):
            sp.dma_start(enc_w[:], io["enc_W"]).then_inc(enc_in, 16)
            sp.dma_start(enc_b[HID:128, :], io["enc_b"]).then_inc(enc_in, 16)
            sp.dma_start(w1_nodes[HID:128], io["w1_nodes"]).then_inc(enc_in, 16)
            for s in range(2):
                sp.dma_start(x_t[s][:], io["x_t"][s]).then_inc(xt_in[s], 16)
            sp.dma_start(dst_steps, io["dst_steps"]).then_inc(steps_in, 16)
            sp.dma_start(dst_i[:], io["dst"]).then_inc(dst_in, 16)
            sp.dma_start(w2t_b2[:], io["w2t_b2"]).then_inc(weights_in, 16)
            sp.dma_start(wih[:], io["wih"]).then_inc(weights_in, 16)
            sp.wait_ge(reduced, 1)
            with nc.allow_non_contiguous_dma(reason="two numbers for each partition, once"):
                for k in range(2):
                    sp.dma_start(range_tab[k:k + 1, :].rearrange("o (p j) -> (o p) j", j=2),
                                 low_high[:, k, :]).then_inc(range_out, 16)
            sp.wait_ge(range_out, 32)
            sp.dma_start(base_all[:], range_tab[0:1, :].to_broadcast([128, STEPS])).then_inc(range_in, 16)
            sp.dma_start(base_f[:], range_tab[0:1, :]).then_inc(range_in, 16)
            sp.dma_start(high_f[:], range_tab[1:2, :]).then_inc(range_in, 16)

            with sp.Fori(0, ENC_SLOT - 1) as i:
                for s in range(2):
                    sp.wait_ge(enc_ps, done(i * 2 + s))
                    settle(sp)
                    sp.dma_start(x_t[s][:], io["x_t"][bass.ds(i * 2 + s + 2, 1)].rearrange("o f n -> (o f) n")).then_inc(xt_in[s], 16)
            sp.wait_ge(setup, 1)
            sp.dma_start(gate_w[HID:128, :, 0:2 * HID], io["whh"][:, :, 0:2 * HID]).then_inc(weights_in, 16)
            sp.dma_start(gate_w[HID:128, :, 3 * HID:4 * HID], io["whh"][:, :, 2 * HID:3 * HID]).then_inc(weights_in, 16)
            sp.dma_start(bias_zr[:], io["bih"][0:128, :]).then_inc(weights_in, 16)
            sp.dma_start(bias_hzr[:], io["bhh"][0:128, :]).then_inc(weights_in, 16)
            sp.dma_start(bias_in[:], io["bih"][128:192, :]).then_inc(weights_in, 16)
            sp.dma_start(bias_hn[HID:128, :], io["bhh"][128:192, :]).then_inc(weights_in, 16)
            sp.dma_start(ro_w1[HID:128, :], io["ro_W1"]).then_inc(weights_in, 16)
            sp.dma_start(ro_b1[:], io["ro_b1"]).then_inc(weights_in, 16)
            sp.dma_start(ro_w2b[:], io["ro_w2b"]).then_inc(weights_in, 16)
            for s in range(2):
                sp.dma_start(source[WINDOW:KEDGE, :, s, :], io["w1_edge"]).then_inc(weights_in, 16)
            sp.wait_ge(cleared, 1)
            for l in range(LAYERS):
                sp.dma_start(q_tab[l][NPAD:NWIN, :], zeros[0:WINDOW, 0:HID]).then_inc(zero_rows, 16)
            passes, slow = load_flags(sp)

            def lead(l, m, k, g, s):
                sp.wait_ge(added, slot_free(k, GATHER_SLOTS))
                settle(sp)
                sp.dma_start(idx[s][:], io["src"][bass.ds(m, 1)].rearrange("o p g -> (o p) g")).then_inc(idx_in[s], 16)

            def front(l, m, k, g, s):
                s = s % 2
                if isinstance(m, int) and m == 0:
                    all_stored(sp, l)
                sp.wait_ge(combined, slot_free(k))
                settle(sp)
                sp.dma_start(pick[s][WINDOW:FEATS, :], io["edge_t"][bass.ds(m, 1)].rearrange("o d e -> (o d) e")).then_inc(edge_in[s], 16)
                base = sp.value_load(base_i[0:1, bass.ds(m, 1)], min_val=0, max_val=NODES)
                sp.dma_start(source[0:WINDOW, l, s, :], q_tab[l][bass.ds(base, WINDOW), :]).then_inc(edge_in[s], 16)

            def end_pass(l, w, k):
                sp.sem_inc(pass_read, 1)
                sp.wait_ge(windows, (passes + 1) * l + w + 2)
                settle(sp)

            def end_passes(l):
                sp.wait_ge(windows, (passes + 1) * (l + 1) + 1)
                settle(sp)

            def chunk_stage(l, j, c, s, last):
                if l == LAYERS - 1 and j == 2:
                    sp.wait_ge(norm, c * NORM_OPS + 1)
                    settle(sp)
                    sp.dma_start(x_rows[:], chunk_rows(io["x_pad"], c)).then_inc(xr_in, 16)

            sp.wait_ge(zero_rows, 16 * LAYERS)
            for l in range(LAYERS):
                run_layer(sp, l, passes, slow, lead, front, None, None, chunk_stage, end_pass, end_passes)

        @block.gpsimd
        def _(pool):
            nc.gpsimd.memset(ident[:], 1.0).then_inc(consts, 1)
            nc.gpsimd.iota(iota_i[:], pattern=[[1, WINDOW]], base=0, channel_multiplier=0)
            nc.gpsimd.iota(stair_i[:], pattern=[[CHUNK, LOOPS], [0, LOOP_STEPS]], base=0, channel_multiplier=0)
            nc.gpsimd.iota(rungs_i[:], pattern=[[WINDOW, MAX_PASSES]], base=0, channel_multiplier=0)
            pool.wait_ge(consts, 1)
            nc.gpsimd.affine_select(out=ident[:], in_=ident[:], compare_op=ALU.is_equal, fill=0.0, base=0,
                                    pattern=[[-1, 128]], channel_multiplier=1).then_inc(consts, 1)
            pool.wait_ge(consts, 2)
            nc.gpsimd.memset(state[0:HID, :], 0.0).then_inc(sums_clear, 1)
            pool.wait_ge(sums_clear, 1)
            pool.wait_ge(reduced, 1)
            nc.gpsimd.memset(degree[HID:HID + 1, :], 0.0).then_inc(sums_clear, 1)
            passes, slow = load_flags(pool)

            def lead(l, m, k, g, s):
                pool.wait_ge(idx_in[s], arrivals(k, s, 16, GATHER_SLOTS))
                pool.wait_ge(added, slot_free(k, GATHER_SLOTS))
                settle(pool)
                for g in range(EDGE_TILES):
                    pool.indirect_dma_start(
                        out=p_src[s][:, g, :], out_offset=None, in_=p_tab[l],
                        in_offset=bass.IndirectOffsetOnAxis(ap=idx[s][:, g:g + 1], axis=0)).then_inc(gathered[s], 16)

            def end_pass(l, w, k):
                pool.wait_ge(added, done(k))
                settle(pool)
                pool.inc_swdge_sem(gathered, [16 * EDGE_TILES * STEPS // GATHER_SLOTS] * GATHER_SLOTS, mode="sub")
                pool.sem_inc(pass_read, 1)

            for l in range(LAYERS):
                all_stored(pool, l)
                run_layer(pool, l, passes, slow, lead, end_pass=end_pass)

        @block.tensor
        def _(pe):
            pe.sem_inc(enc_ps, CREDIT)
            pe.sem_inc(enc_projected, CREDIT)
            pe.sem_inc(flipped, CREDIT)
            pe.sem_inc(combined, CREDIT)
            pe.sem_inc(scattered, CREDIT)
            pe.sem_inc(projected, 1)
            pe.sem_inc(hid_ps, 1)

            def enc_hidden(c, s, n_in):
                pe.wait_ge(xt_in[s], n_in)
                pe.wait_ge(enc_h, slot_free(c))
                settle(pe)
                nc.tensor.matmul(enc_h_ps[s][HID:128, 0:CHUNK], enc_w[:], x_t[s][:], start=True, stop=True).then_inc(enc_ps, 1)

            def enc_project(c, s):
                pe.wait_ge(enc_h, done(c))
                pe.wait_ge(enc_staged, slot_free(c))
                hn = h_enc[s][:].rearrange("q (p j) -> q j p", j=4)
                for j in range(4):
                    last = nc.tensor.matmul(enc_pq_ps[s][0:CPART, j * 128:(j + 1) * 128], hn[HID:128, j, :],
                                            w1_nodes[HID:128, 0, :], start=True, stop=True)
                last.then_inc(enc_projected, 1)

            pe.wait_ge(enc_in, 48)
            for c in range(2):
                enc_hidden(c, c, 16)
            with pe.Fori(0, ENC_SLOT - 1) as i:
                for s in range(2):
                    enc_project(i * 2 + s, s)
                    enc_hidden(i * 2 + s + 2, s, i * 16 + 32)
            for c in (CHUNKS - 2, CHUNKS - 1):
                enc_project(c, c % 2)
            pe.wait_ge(weights_in, 16 * 13)
            for l in range(LAYERS):
                pe.wait_ge(enc_h, done(CHUNKS - 1))
                if l:
                    pe.wait_ge(vw_sb, l)
                nc.tensor.matmul(zr_ps[0:HID + 1, 0:3 * HID], w2t_b2[:, l, :], wih[:, l, :], start=True, stop=True).then_inc(vw_ps, 1)
            pe.wait_ge(vw_sb, LAYERS)
            pe.wait_ge(cleared, 1)
            pe.wait_ge(consts, 2)
            pe.wait_ge(enc_staged, done(CHUNKS - 1))
            passes, slow = load_flags(pe)

            def lead(l, m, k, g, s):
                s = s % 2
                pe.wait_ge(hot_t_ready, done(k))
                pe.wait_ge(pick_ready, single_free(k))
                for g in range(EDGE_TILES):
                    last = nc.tensor.transpose(hott_ps[0:WINDOW, g * 128:(g + 1) * 128], hot_t[s][:, g, :], ident[:])
                last.then_inc(flipped, 1)

            def front(l, m, k, g, s):
                s = s % 2
                pe.wait_ge(pick_ready, done(k))
                pe.wait_ge(edge_in[s], arrivals(k, s, 32))
                pe.wait_ge(added, slot_free(k))
                for g in range(EDGE_TILES):
                    last = nc.tensor.matmul(pre_ps[s][:, g, :], pick[s][0:KEDGE, g * 128:(g + 1) * 128],
                                            source[0:KEDGE, l, s, :], start=True, stop=True)
                last.then_inc(combined, 1)

            def back(l, m, k, g, s):
                s = s % 2
                pe.wait_ge(hot_ready, done(k))
                pe.wait_ge(msg_ready, done(k))
                pe.wait_ge(summed, single_free(k))
                for g in range(EDGE_TILES):
                    last = nc.tensor.matmul(sum_ps[0:HID + 1, 0:WINDOW], msg[s][:, g, :], hot[s][:, g, :],
                                            start=(g == 0), stop=(g == EDGE_TILES - 1))
                last.then_inc(scattered, 1)

            def chunk_stage(l, j, c, s, last):
                n = before(l, c)
                if j == 0:
                    pe.wait_ge(chunk_in, n + 1)
                    if l == LAYERS - 1:
                        pe.wait_ge(hid_ready, c + 1 - two_slots(c))
                    for ps, g in zip(gate_ps[s], (0, 2 * HID)):
                        nc.tensor.matmul(ps[:, 0:CHUNK], gate_w[:, l, g:g + 128], chunk[s][:], start=True, stop=False)
                        end = nc.tensor.matmul(ps[:, 0:CHUNK], deg_w[HID:HID + 1, l, g:g + 128],
                                               chunk_deg[s][HID:HID + 1, :], start=False, stop=True)
                    end.then_inc(gates_ps, 1)
                if j == 3:
                    pe.wait_ge(gru, GRU_OPS * (n + 1) + 1)
                    if l < LAYERS - 1:
                        pe.wait_ge(staged, n + 1)
                        hn = h_next[:].rearrange("q (p j) -> q j p", j=4)
                        for q in range(4):
                            end = nc.tensor.matmul(pq_ps[0:CPART, q * 128:(q + 1) * 128], hn[HID:128, q, :],
                                                   w1_nodes[HID:128, l + 1, :], start=True, stop=True)
                        end.then_inc(projected, 1)
                    else:
                        settle(pe)
                        nc.tensor.matmul(gate_ps[s][0][0:HID, 0:CHUNK], ro_w1[HID:128, :], h_next[HID:128, :],
                                         start=True, stop=True).then_inc(hid_ps, 1)
                if j == 4 and l == LAYERS - 1:
                    pe.wait_ge(hid_ready, c + 2)
                    pe.wait_ge(norm, c * NORM_OPS + 1)
                    hv = hid[:].rearrange("q (p j) -> q j p", j=4)
                    for q in range(4):
                        end = nc.tensor.matmul(pq_ps[0:CPART, q * HID:(q + 1) * HID], hv[:, q, :], ro_w2b[:],
                                               start=True, stop=True)
                    end.then_inc(y_ps, 1)

            for l in range(LAYERS):
                if l == LAYERS - 1:
                    pe.wait_ge(staged, CHUNKS * l + 1)
                run_layer(pe, l, passes, slow, lead, front, back, None, chunk_stage)

        @block.scalar
        def _(act):
            for credit in (enc_kept, enc_staged):
                act.sem_inc(credit, CREDIT)

            def enc_chunk(c, s, n_stored):
                act.wait_ge(enc_h, done(c))
                nc.scalar.copy(state[HID:128, cols(c)], h_enc[s][HID:128, :]).then_inc(enc_kept, 1)
                act.wait_ge(enc_projected, done(c))
                if n_stored is not None:
                    act.wait_ge(stored[s], n_stored)
                nc.scalar.copy(stage[s][:].rearrange("p t j f -> p j t f"), pq_view(enc_pq_ps[s])).then_inc(enc_staged, 1)
                act.wait_ge(enc_staged, done(c))
                act.dma_start(chunk_rows(p_tab[0], c), stage[s][:, 0]).then_inc(stored[s], 16)
                act.dma_start(chunk_rows(q_tab[0][0:NPAD, :], c), stage[s][:, 1]).then_inc(stored[s], 16)

            for c in range(2):
                enc_chunk(c, c, None)
            with act.Fori(1, ENC_SLOT) as i:
                for s in range(2):
                    enc_chunk(i * 2 + s, s, i * 32)
            act.wait_ge(setup, 1)
            for l in range(LAYERS):
                act.wait_ge(vw_ps, l + 1)
                nc.scalar.copy(gate_w[0:HID, l, 0:3 * HID], zr_ps[0:HID, 0:3 * HID])
                nc.scalar.copy(deg_w[HID:HID + 1, l, 0:3 * HID], zr_ps[HID:HID + 1, 0:3 * HID]).then_inc(vw_sb, 1)
            passes, slow = load_flags(act)
            act.wait_ge(cleared, 1)
            act.wait_ge(bias_ready, 1)
            for credit in (pick_ready, msg_ready):
                act.sem_inc(credit, CREDIT)
            for credit in (staged, h_kept, hid_ready):
                act.sem_inc(credit, 1)
            act.wait_ge(enc_kept, done(CHUNKS - 1))

            def lead(l, m, k, g, s):
                s = s % 2
                act.wait_ge(flipped, done(k))
                act.wait_ge(combined, slot_free(k))
                nc.scalar.copy(pick[s][0:WINDOW, :], hott_ps[0:WINDOW, :]).then_inc(pick_ready, 1)

            def back(l, m, k, g, s):
                s = s % 2
                act.wait_ge(added, done(k))
                act.wait_ge(scattered, slot_free(k))
                nc.scalar.activation(msg[s][:, :, 0:HID], pre[s][:], ACT.Relu).then_inc(msg_ready, 1)

            def chunk_stage(l, j, c, s, last):
                n = before(l, c)
                if j == 0:
                    act.wait_ge(summed, done(last))
                    act.wait_ge(gru, (n - two_slots(c)) * GRU_OPS + 1)
                    if l:
                        act.wait_ge(h_kept, CHUNKS * l + 1)
                    nc.scalar.copy(chunk[s][:], state[:, cols(c)])
                    nc.scalar.copy(chunk_deg[s][HID:HID + 1, :], degree[HID:HID + 1, cols(c)]).then_inc(chunk_in, 1)
                if j == 1:
                    act.wait_ge(gates_ps, n + 1)
                    nc.scalar.activation(zr[s][:], gate_ps[s][0][:, 0:CHUNK], ACT.Sigmoid, bias=bias_zr[:, l:l + 1]).then_inc(zr_ready, 1)
                if j == 2:
                    act.wait_ge(gru, GRU_OPS * n + 4)
                    nc.scalar.activation(n_hi[HID:128, :], npre[:], ACT.Tanh, bias=bias_in[:, l:l + 1]).then_inc(n_ready, 1)
                if j == 3 and l < LAYERS - 1:
                    act.wait_ge(gru, GRU_OPS * (n + 1) + 1)
                    nc.scalar.copy(state[HID:128, cols(c)], h_next[HID:128, :]).then_inc(h_kept, 1)
                if j == 4 and l < LAYERS - 1:
                    act.wait_ge(projected, n + 2)
                    act.wait_ge(stored[s], stored_before(l, c, s))
                    nc.scalar.copy(stage[s][:].rearrange("p t j f -> p j t f"), pq_view(pq_ps)).then_inc(staged, 1)
                    act.wait_ge(staged, n + 2)
                    act.dma_start(chunk_rows(p_tab[l + 1], c), stage[s][:, 0]).then_inc(stored[s], 16)
                    act.dma_start(chunk_rows(q_tab[l + 1][0:NPAD, :], c), stage[s][:, 1]).then_inc(stored[s], 16)
                if j == 4 and l == LAYERS - 1:
                    act.wait_ge(hid_ps, c + 2)
                    act.wait_ge(norm, c * NORM_OPS + 1)
                    nc.scalar.activation(hid[0:HID, :], gate_ps[s][0][0:HID, 0:CHUNK], ACT.Relu, bias=ro_b1[:]).then_inc(hid_ready, 1)
                if j == 6 and l == LAYERS - 1:
                    act.wait_ge(norm, c * NORM_OPS + 8)
                    nc.scalar.activation(sd[:], veps[:], ACT.Sqrt).then_inc(sd_ready, 1)
                if j == 7 and l == LAYERS - 1:
                    act.wait_ge(norm, (c + 1) * NORM_OPS + 1)
                    if isinstance(c, int) and c == CHUNKS - 1:
                        act.dma_start(io["out"][c * CHUNK:NODES, :].rearrange("(p j) f -> p j f", j=4),
                                      y_out[0:LAST_PART]).then_inc(out_done, 16)
                    else:
                        act.dma_start(chunk_rows(io["out"][0:(CHUNKS - 1) * CHUNK, :], c), y_out[:]).then_inc(out_done, 16)

            for l in range(LAYERS):
                run_layer(act, l, passes, slow, lead, None, back, None, chunk_stage)
            act.wait_ge(out_done, 16 * CHUNKS)

        @block.vector
        def _(dve):
            for credit in (enc_h, hot_t_ready, hot_ready, added, summed):
                dve.sem_inc(credit, CREDIT)
            dve.sem_inc(gru, 1)
            dve.sem_inc(norm, 1)
            nc.vector.memset(gate_w[:], 0.0)
            nc.vector.memset(deg_w[:], 0.0).then_inc(setup, 1)
            dve.wait_ge(steps_in, 16)
            nc.vector.tensor_reduce(low_high[:, 0, :], dst_steps, AX.X, ALU.min)
            nc.vector.tensor_reduce(low_high[:, 1, :], dst_steps, AX.X, ALU.max).then_inc(reduced, 1)
            nc.vector.memset(zeros[:], 0.0)
            nc.vector.memset(hid[HID:HID + 1, :], 1.0)
            for s in range(2):
                nc.vector.memset(pick[s][WINDOW:128, :], 1.0)
                last = nc.vector.memset(msg[s][:], 1.0)
            last.then_inc(cleared, 1)

            def enc_chunk(c, s):
                dve.wait_ge(enc_ps, done(c))
                dve.wait_ge(enc_kept, slot_free(c))
                dve.wait_ge(enc_projected, slot_free(c))
                nc.vector.tensor_scalar(h_enc[s][HID:128, :], enc_h_ps[s][HID:128, 0:CHUNK], enc_b[HID:128, :],
                                        None, ALU.add).then_inc(enc_h, 1)

            dve.wait_ge(enc_in, 48)
            for c in range(2):
                enc_chunk(c, c)

            chain = [1]

            def link(op):
                chain[0] += 1
                op.then_inc(setup, 1)
                dve.wait_ge(setup, chain[0])

            dve.wait_ge(consts, 2)
            nc.vector.tensor_copy(iota_ps, iota_i[:])
            nc.vector.tensor_copy(stair[:], stair_i[:])
            link(nc.vector.tensor_copy(rungs[:], rungs_i[:]))
            dve.wait_ge(dst_in, 16)
            dve.wait_ge(range_in, 48)
            nc.vector.tensor_tensor(rel[:], dst_i[:], base_all[:].unsqueeze(2).to_broadcast([128, STEPS, EDGE_TILES]), ALU.subtract)
            nc.vector.tensor_copy(start_f[:], base_f[:])
            nc.vector.tensor_scalar(base_i[:], base_f[:], float(NODES), None, ALU.min)
            nc.vector.tensor_tensor(late[:], base_f[:], stair[:], ALU.is_lt)
            link(nc.vector.tensor_tensor(spread[:], high_f[:], base_f[:], ALU.subtract))
            nc.vector.tensor_reduce(late_n[:], late[:], AX.X, ALU.add)
            link(nc.vector.tensor_reduce(widest[:], spread[:], AX.X, ALU.max))
            link(nc.vector.tensor_scalar(reach[:], rungs[:], widest[0:1, 0:1], None, ALU.is_le))
            link(nc.vector.tensor_reduce(passes_f[:], reach[:], AX.X, ALU.add))
            link(nc.vector.scalar_tensor_tensor(slow_f[:], passes_f[:], -1.0, late_n[:], ALU.add, ALU.add))
            nc.vector.tensor_copy(flags[0:1, 0:1], passes_f[:])
            nc.vector.tensor_copy(flags[0:1, 1:2], slow_f[:]).then_inc(windows, 1)

            with dve.Fori(1, ENC_SLOT) as i:
                for s in range(2):
                    enc_chunk(i * 2 + s, s)
            dve.wait_ge(weights_in, 16 * 13)
            nc.vector.tensor_tensor(bias_zr[:], bias_zr[:], bias_hzr[:], ALU.add).then_inc(bias_ready, 1)
            dve.wait_ge(sums_clear, 2)
            passes, slow = load_flags(dve)

            def rel_of(m):
                return rel[:, bass.ds(m, 1), :].rearrange("p o g -> p (o g)").unsqueeze(2).to_broadcast([128, EDGE_TILES, WINDOW])

            node = iota_ps.unsqueeze(1).to_broadcast([128, EDGE_TILES, WINDOW])

            def lead(l, m, k, g, s):
                s = s % 2
                dve.wait_ge(flipped, slot_free(k))
                nc.vector.tensor_tensor(hot_t[s][:], rel_of(m), node, ALU.is_equal).then_inc(hot_t_ready, 1)

            def front(l, m, k, g, s):
                s = s % 2
                dve.wait_ge(scattered, slot_free(k))
                nc.vector.tensor_tensor(hot[s][:], rel_of(m), node, ALU.is_equal).then_inc(hot_ready, 1)

            def back(l, m, k, g, s):
                r, s = s, s % 2
                dve.wait_ge(gathered[r], arrivals(g, r, 16 * EDGE_TILES, GATHER_SLOTS))
                dve.wait_ge(combined, done(k))
                dve.wait_ge(msg_ready, slot_free(k))
                nc.vector.tensor_tensor(pre[s][:], pre_ps[s][:], p_src[r][:], ALU.add).then_inc(added, 1)

            def trail(l, m, k, g, s):
                base = dve.value_load(base_i[0:1, bass.ds(m, 1)], min_val=0, max_val=NODES)
                dve.wait_ge(scattered, done(k))
                dve.wait_ge(summed, single_free(k))
                here = bass.ds(base, WINDOW)
                nc.vector.tensor_tensor(state[0:HID, here], sum_ps[0:HID, 0:WINDOW], state[0:HID, here], ALU.add)
                nc.vector.tensor_tensor(degree[HID:HID + 1, here], sum_ps[HID:HID + 1, 0:WINDOW],
                                        degree[HID:HID + 1, here], ALU.add).then_inc(summed, 1)

            def end_pass(l, w, k):
                dve.wait_ge(hot_ready, done(k))
                dve.wait_ge(pass_read, (passes * l + w + 1) * 2)
                nc.vector.tensor_scalar(rel[:], rel[:], float(-WINDOW), None, ALU.add)
                nc.vector.tensor_scalar(start_f[:], start_f[:], float(WINDOW), None, ALU.add).then_inc(window_step, 1)
                dve.wait_ge(window_step, (passes + 1) * l + w + 1)
                nc.vector.tensor_scalar(base_i[:], start_f[:], float(NODES), None, ALU.min).then_inc(windows, 1)
                dve.wait_ge(windows, (passes + 1) * l + w + 2)
                settle(dve)

            def end_passes(l):
                nc.vector.tensor_tensor(rel[:], dst_i[:], base_all[:].unsqueeze(2).to_broadcast([128, STEPS, EDGE_TILES]), ALU.subtract)
                nc.vector.tensor_copy(start_f[:], base_f[:]).then_inc(window_step, 1)
                nc.vector.tensor_scalar(base_i[:], base_f[:], float(NODES), None, ALU.min).then_inc(windows, 1)
                dve.wait_ge(windows, (passes + 1) * (l + 1) + 1)
                settle(dve)

            def chunk_stage(l, j, c, s, last):
                n = before(l, c)
                g0 = GRU_OPS * n + 1
                if j == 1:
                    dve.wait_ge(chunk_in, n + 1)
                    dve.wait_ge(summed, done(last))
                    nc.vector.tensor_copy(state[0:HID, cols(c)], zeros[0:HID, :])
                    nc.vector.tensor_copy(degree[HID:HID + 1, cols(c)], zeros[HID:HID + 1, :]).then_inc(gru, 1)
                    dve.wait_ge(zr_ready, n + 1)
                    nc.vector.scalar_tensor_tensor(rn[:], gate_ps[s][1][HID:128, 0:CHUNK], bias_hn[HID:128, l:l + 1], zr[s][HID:128, :],
                                                   ALU.add, ALU.mult).then_inc(gru, 1)
                    dve.wait_ge(gru, g0 + 2)
                    nc.vector.tensor_tensor(npre[:], gate_ps[s][1][0:HID, 0:CHUNK], rn[:], ALU.add).then_inc(gru, 1)
                if j == 2:
                    dve.wait_ge(n_ready, n + 1)
                    nc.vector.tensor_tensor(diff[:], chunk[s][HID:128, :], n_hi[HID:128, :], ALU.subtract).then_inc(gru, 1)
                    dve.wait_ge(gru, g0 + 4)
                    nc.vector.tensor_tensor(zdiff[HID:128, :], zr[s][0:HID, :], diff[:], ALU.mult).then_inc(gru, 1)
                    dve.wait_ge(gru, g0 + 5)
                    if l < LAYERS - 1:
                        dve.wait_ge(projected, n + 1)
                        dve.wait_ge(h_kept, n + 1)
                    else:
                        dve.wait_ge(hid_ps, c + 1)
                    nc.vector.tensor_tensor(h_next[HID:128, :], n_hi[HID:128, :], zdiff[HID:128, :], ALU.add).then_inc(gru, 1)
                if j == 5 and l == LAYERS - 1:
                    n0 = c * NORM_OPS + 1
                    dve.wait_ge(y_ps, c + 1)
                    dve.wait_ge(xr_in, c * 16 + 16)
                    nc.vector.tensor_tensor(y[:], pq_ps[0:CPART, 0:4 * HID].rearrange("p (j f) -> p j f", j=4), x_rows[:], ALU.add).then_inc(norm, 1)
                    dve.wait_ge(norm, n0 + 1)
                    nc.vector.tensor_reduce(ysum[:], y[:], AX.X, ALU.add).then_inc(norm, 1)
                    dve.wait_ge(norm, n0 + 2)
                    nc.vector.tensor_scalar(ymean[:], ysum[:], 1.0 / HID, None, ALU.mult).then_inc(norm, 1)
                    dve.wait_ge(norm, n0 + 3)
                    nc.vector.tensor_tensor(yc[:], y[:], ymean[:].unsqueeze(2).to_broadcast([CPART, 4, HID]), ALU.subtract).then_inc(norm, 1)
                    dve.wait_ge(norm, n0 + 4)
                    nc.vector.tensor_tensor(ysq[:], yc[:], yc[:], ALU.mult).then_inc(norm, 1)
                    dve.wait_ge(norm, n0 + 5)
                    nc.vector.tensor_reduce(vsum[:], ysq[:], AX.X, ALU.add).then_inc(norm, 1)
                    dve.wait_ge(norm, n0 + 6)
                    nc.vector.tensor_scalar(veps[:], vsum[:], 1.0 / HID, EPS, ALU.mult, ALU.add).then_inc(norm, 1)
                if j == 6 and l == LAYERS - 1:
                    n0 = c * NORM_OPS + 1
                    dve.wait_ge(sd_ready, c + 1)
                    nc.vector.reciprocal(rstd[:], sd[:]).then_inc(norm, 1)
                    dve.wait_ge(norm, n0 + 8)
                    if isinstance(c, int) and c == 0:
                        pass
                    else:
                        dve.wait_ge(out_done, c * 16)
                    nc.vector.tensor_tensor(y_out[:], yc[:], rstd[:].unsqueeze(2).to_broadcast([CPART, 4, HID]), ALU.mult).then_inc(norm, 1)

            for l in range(LAYERS):
                if l:
                    dve.wait_ge(gru, GRU_OPS * CHUNKS * l + 1)
                run_layer(dve, l, passes, slow, lead, front, back, trail, chunk_stage, end_pass, end_passes)


def kernel(**inputs):
    import numpy as np
    import concourse.bacc as bacc
    from concourse.bass_utils import run_bass_kernel_spmd

    a = {k.replace("L0_gnn_", ""): np.asarray(v) for k, v in inputs.items()}
    padded = STEPS * STEP

    def pad(v, n, fill=0):
        out = np.full((n,) + v.shape[1:], fill, v.dtype)
        out[:len(v)] = v
        return out

    src = pad(a["src"], padded).reshape(STEPS, EDGE_TILES, 128)
    dst = pad(a["dst"], padded, NODES)
    edge = pad(a["edge_attr_16"], padded)
    x = pad(a["x"], NPAD)

    def gates(v):
        return v.reshape(v.shape[:-1] + (3, HID))[..., [1, 0, 2], :].reshape(v.shape)

    w1 = a["msg_W1"]
    arrays = {
        "x_t": x.reshape(CHUNKS, CHUNK, HID).transpose(0, 2, 1),
        "x_pad": x,
        "src": src.transpose(0, 2, 1),
        "dst": dst.reshape(STEPS, EDGE_TILES, 128).transpose(2, 0, 1),
        "dst_steps": dst.reshape(STEPS // 2, 2, STEP),
        "edge_t": edge.reshape(STEPS, STEP, EDGE_DIM).transpose(0, 2, 1),
        "enc_W": a["enc_W"],
        "enc_b": a["enc_b"][:, None],
        "w1_nodes": np.concatenate([w1[:, :HID], w1[:, HID:2 * HID]], 2).transpose(1, 0, 2),
        "w1_edge": np.concatenate([w1[:, 2 * HID:], a["msg_b1"][:, None]], 1).transpose(1, 0, 2),
        "w2t_b2": np.concatenate([a["msg_W2"], a["msg_b2"][:, None]], 1).transpose(2, 0, 1),
        "wih": gates(a["gru_Wih"]).transpose(1, 0, 2),
        "whh": gates(a["gru_Whh"]).transpose(1, 0, 2),
        "bih": gates(a["gru_bih"]).T,
        "bhh": gates(a["gru_bhh"]).T,
        "ro_W1": a["ro_W1"],
        "ro_b1": a["ro_b1"][:, None],
        "ro_w2b": np.concatenate([a["ro_W2"], a["ro_b2"][None]], 0),
    }
    nc = bacc.Bacc("TRN2", target_bir_lowering=False, num_devices=1)
    io = {}
    for name, v in arrays.items():
        arrays[name] = v = np.ascontiguousarray(v)
        dt = U32 if name == "src" else I32 if name.startswith("dst") else F32
        if name == "src":
            arrays[name] = v = v.view(np.uint32)
        io[name] = nc.dram_tensor(f"in_{name}", v.shape, dt, kind="ExternalInput").ap()
    io["out"] = nc.dram_tensor("out", (NODES, HID), F32, kind="ExternalOutput").ap()
    build(nc, io)
    result = run_bass_kernel_spmd(nc, [{f"in_{k}": v for k, v in arrays.items()}], core_ids=[0])
    return result.results[0]["out"]
```

```python
import concourse.bass as bass
from concourse import mybir
from contextlib import ExitStack

F32 = mybir.dt.float32
BF16 = mybir.dt.bfloat16
I32 = mybir.dt.int32
U32 = mybir.dt.uint32
ALU = mybir.AluOpType
ACT = mybir.ActivationFunctionType
AX = mybir.AxisListType

LAYERS = 3
HID = 64
EDGE_DIM = 16
NODES = 12500
EDGES = 212500
EDGE_TILES = 8
STEP = EDGE_TILES * 128
STEPS = -(-EDGES // STEP)
WINDOW = 96
FEATS = WINDOW + EDGE_DIM
KEDGE = FEATS + 1
LOOP_STEPS = 8
LOOPS = STEPS // LOOP_STEPS
CHUNK = 468
CPART = CHUNK // 4
CHUNKS = -(-NODES // CHUNK)
LOOPED = CHUNKS - 1
HALF = LOOP_STEPS // 2
NPAD = CHUNKS * CHUNK
NWIN = NPAD + WINDOW
MAX_PASSES = NODES // WINDOW + 1
LAST_NODES = NODES - (CHUNKS - 1) * CHUNK
LAST_PARTS = -(-LAST_NODES // 8) * 2
NLAST = (CHUNKS - 1) * CHUNK + LAST_PARTS * 4
GATHER_SLOTS = 4
CREDIT = GATHER_SLOTS
PAIRS = CHUNKS // 2
X_PIECES = [(0, 2), (2, 10), (10, CHUNKS)]
SETUP_PAIR = 8
WEIGHTS = 15
ONES = 5
assert CHUNKS == 2 * PAIRS + 1 and LOOPED == LOOPS
GRU_OPS = 6
NORM_OPS = 9
EPS = 1e-5


def build(nc, io):
    with ExitStack() as ctx:
        def sb(name, shape, dt=F32):
            return ctx.enter_context(nc.sbuf_tensor(name, shape, dt))

        def sem(name):
            return ctx.enter_context(nc.semaphore(name))

        p_tab = [nc.dram_tensor(f"p_tab{l}", [NPAD, HID], F32).ap() for l in range(LAYERS)]
        q_tab = [nc.dram_tensor(f"q_tab{l}", [NWIN, HID], F32).ap() for l in range(LAYERS)]
        range_tab = nc.dram_tensor("range_tab", [2, STEPS], F32).ap()

        ident = sb("ident", [128, 128], BF16)
        zeros = sb("zeros", [128, CHUNK])
        iota_i = sb("iota_i", [128, WINDOW], I32)
        stair_i = sb("stair_i", [1, STEPS], I32)
        stair = sb("stair", [1, STEPS])
        rungs_i = sb("rungs_i", [1, MAX_PASSES], I32)
        rungs = sb("rungs", [1, MAX_PASSES])
        enc_w = sb("enc_w", [128, HID])
        enc_b = sb("enc_b", [128, 1])
        enc_wt_b = sb("enc_wt_b", [128, HID + 1])
        enc_w1 = sb("enc_w1", [HID + 1, 2 * HID])
        w1_nodes = sb("w1_nodes", [128, LAYERS, 2 * HID])
        w2t_b2 = sb("w2t_b2", [HID, LAYERS, HID + 1])
        wih = sb("wih", [HID, LAYERS, 3 * HID])
        gate_w = sb("gate_w", [128, LAYERS, 4 * HID])
        sum_w = sb("sum_w", [HID + 1, LAYERS, 4 * HID])
        bias_zr = sb("bias_zr", [128, LAYERS])
        bias_hzr = sb("bias_hzr", [128, LAYERS])
        bias_in = sb("bias_in", [HID, LAYERS])
        bias_hn = sb("bias_hn", [128, LAYERS])
        ro_w1 = sb("ro_w1", [128, HID])
        ro_b1 = sb("ro_b1", [HID, 1])
        ro_w2b = sb("ro_w2b", [HID + 1, HID])
        low_high = sb("low_high", [STEPS // 2, 2, 2])
        dst_i = sb("dst_i", [128, STEPS, EDGE_TILES], I32)
        base_all = sb("base_all", [128, STEPS])
        rel = sb("rel", [128, STEPS, EDGE_TILES])
        base_f = sb("base_f", [1, STEPS])
        high_f = sb("high_f", [1, STEPS])
        spread = sb("spread", [1, STEPS])
        late = sb("late", [1, STEPS])
        start_f = sb("start_f", [1, STEPS])
        base_i = sb("base_i", [1, STEPS], I32)
        widest = sb("widest", [1, 1])
        reach = sb("reach", [1, MAX_PASSES])
        passes_f = sb("passes_f", [1, 1])
        late_n = sb("late_n", [1, 1])
        slow_f = sb("slow_f", [1, 1])
        flags = sb("flags", [1, 2], I32)
        state = sb("state", [128, NWIN])
        sums = sb("sums", [128, NWIN])
        dst_steps = sums[0:STEPS // 2, 0:2 * STEP].bitcast(I32).rearrange("p (j e) -> p j e", j=2)
        idx = [sb(f"idx{s}", [128, EDGE_TILES], U32) for s in range(GATHER_SLOTS)]
        p_src = [sb(f"p_src{s}", [128, EDGE_TILES, HID]) for s in range(GATHER_SLOTS)]
        hot_t = [sb(f"hot_t{s}", [128, EDGE_TILES, WINDOW], BF16) for s in range(2)]
        hot = [sb(f"hot{s}", [128, EDGE_TILES, WINDOW]) for s in range(2)]
        pick = [sb(f"pick{s}", [128, STEP]) for s in range(2)]
        source = sb("source", [128, LAYERS, 2, HID])
        pre = [sb(f"pre{s}", [128, EDGE_TILES, HID]) for s in range(2)]
        msg = [sb(f"msg{s}", [128, EDGE_TILES, HID + 1]) for s in range(2)]
        x_one = [sb(f"x_one{s}", [HID + 1, CHUNK]) for s in range(2)]
        chunk = sb("chunk", [128, CHUNK])
        chunk_sum = sb("chunk_sum", [HID + 1, CHUNK])
        zr = sb("zr", [128, CHUNK])
        rn = sb("rn", [HID, CHUNK])
        npre = sb("npre", [HID, CHUNK])
        n_hi = sb("n_hi", [128, CHUNK])
        diff = sb("diff", [HID, CHUNK])
        zdiff = sb("zdiff", [128, CHUNK])
        h_next = sb("h_next", [128, CHUNK])
        stage = [sb(f"stage{s}", [CPART, 2, 4, HID]) for s in range(2)]
        hid = sb("hid", [HID + 1, CHUNK])
        x_rows = sb("x_rows", [CPART, 4, HID])
        y = sb("y", [CPART, 4, HID])
        yc = sb("yc", [CPART, 4, HID])
        ysq = sb("ysq", [CPART, 4, HID])
        ysum = sb("ysum", [CPART, 4])
        ymean = sb("ymean", [CPART, 4])
        vsum = sb("vsum", [CPART, 4])
        veps = sb("veps", [CPART, 4])
        sd = sb("sd", [CPART, 4])
        rstd = sb("rstd", [CPART, 4])
        y_out = sb("y_out", [CPART, 4, HID])

        bank = [ctx.enter_context(nc.psum_tensor(f"bank{i}", [128, 512], F32)) for i in range(5)]
        iota_ps = bank[0][:, 0:WINDOW]
        sum_ps = bank[1]
        zr_ps, n_ps, pq_ps = bank[2], bank[3], bank[4]
        hott_ps = ctx.enter_context(nc.psum_tensor("hott_ps", [128, STEP], BF16))
        pre_ps = [ctx.enter_context(nc.psum_tensor(f"pre_ps{s}", [128, EDGE_TILES, HID], F32)) for s in range(2)]

        consts = sem("consts")
        dst_in = sem("dst_in")
        steps_in = sem("steps_in")
        weights_in = sem("weights_in")
        reduced = sem("reduced")
        range_out = sem("range_out")
        range_in = sem("range_in")
        setup = sem("setup")
        vw_ps = sem("vw_ps")
        vw_sb = sem("vw_sb")
        zero_rows = sem("zero_rows")
        zeroed = sem("zeroed")
        cleared = sem("cleared")
        sums_clear = sem("sums_clear")
        bias_ready = sem("bias_ready")
        enc_in = sem("enc_in")
        x_in = [sem(f"x_in{q}") for q in range(len(X_PIECES))]
        w1_ps = sem("w1_ps")
        w1_sb = sem("w1_sb")
        enc_x = sem("enc_x")
        enc_projected = sem("enc_projected")
        enc_staged = sem("enc_staged")
        stored = [sem(f"stored{s}") for s in range(2)]
        idx_in = [sem(f"idx_in{s}") for s in range(GATHER_SLOTS)]
        edge_in = [sem(f"edge_in{s}") for s in range(2)]
        pace = sem("pace")
        gathered = [sem(f"gathered{s}") for s in range(GATHER_SLOTS)]
        hot_t_ready = sem("hot_t_ready")
        hot_ready = sem("hot_ready")
        flipped = sem("flipped")
        pick_ready = sem("pick_ready")
        combined = sem("combined")
        added = sem("added")
        msg_ready = sem("msg_ready")
        scattered = sem("scattered")
        summed = sem("summed")
        windows = sem("windows")
        window_step = sem("window_step")
        pass_read = sem("pass_read")
        chunk_h_in = sem("chunk_h_in")
        chunk_in = sem("chunk_in")
        enc_ps = sem("enc_ps")
        enc_h = sem("enc_h")
        gates_ps = sem("gates_ps")
        zr_ready = sem("zr_ready")
        gru = sem("gru")
        n_ready = sem("n_ready")
        h_kept = sem("h_kept")
        projected = sem("projected")
        staged = sem("staged")
        hid_ps = sem("hid_ps")
        hid_ready = sem("hid_ready")
        y_ps = sem("y_ps")
        xr_in = sem("xr_in")
        norm = sem("norm")
        sd_ready = sem("sd_ready")
        out_done = sem("out_done")

        def done(k):
            return k + (CREDIT + 1)

        def slot_free(k, slots=2):
            return k + (CREDIT + 1 - slots)

        def single_free(k):
            return k + CREDIT

        def arrivals(k, s, each, slots=2):
            return (k - s) * (each // slots) + each

        def cols(c):
            return bass.ds(c * CHUNK, CHUNK)

        def before(l, c):
            return c + l * CHUNKS

        def stored_before(l, c):
            return 32 * (c + (PAIRS + 1 + CHUNKS * l))

        def all_stored(eng, l):
            eng.wait_ge(stored[0], 32 * (PAIRS + 1 + CHUNKS * l))
            eng.wait_ge(stored[1], 32 * PAIRS)

        def settle(eng):
            eng.sem_inc(pace, 1)

        def load_flags(eng):
            eng.wait_ge(windows, 1)
            return (eng.value_load(flags[0:1, 0:1], min_val=1, max_val=MAX_PASSES),
                    eng.value_load(flags[0:1, 1:2], min_val=0, max_val=STEPS + MAX_PASSES))

        def run_layer(eng, l, passes, slow, lead=None, front=None, back=None, trail=None, chunk_begin=None,
                      chunk_stage=None, end_pass=None, end_passes=None):
            k0 = 0 if l == 0 else passes * (l * STEPS)
            last = k0 + passes * STEPS - 1

            def part(what, i, k, g, j):
                if what:
                    n = i * LOOP_STEPS + j
                    what(l, n, k + n, g + n, j % GATHER_SLOTS)

            def round_of_steps(i, k, g, with_chunks, first=False, final=False):
                for j in range(LOOP_STEPS):
                    if j + 2 < LOOP_STEPS or not final:
                        part(lead, i, k, g, j + 2)
                    if j + 1 < LOOP_STEPS or not final:
                        part(front, i, k, g, j + 1)
                    if j or not first:
                        part(trail, i, k, g, j - 1)
                    if with_chunks and chunk_stage and final and j == LOOP_STEPS - 1:
                        chunk_begin(l, LOOPED)
                    part(back, i, k, g, j)
                    if with_chunks and chunk_stage:
                        if not final:
                            if j == 0:
                                chunk_begin(l, i - 1)
                            chunk_stage(l, j, i - 1, k + i * LOOP_STEPS - 1)
                        else:
                            half = j // HALF
                            if j % HALF == 0:
                                chunk_begin(l, i - 1 + half)
                            for stage_n in range(2 * (j % HALF), 2 * (j % HALF) + 2):
                                chunk_stage(l, stage_n, i - 1 + half, k + i * LOOP_STEPS + half * HALF - 1)

            def one_pass(k, g, with_chunks):
                part(lead, 0, k, g, 0)
                part(lead, 0, k, g, 1)
                part(front, 0, k, g, 0)
                round_of_steps(0, k, g, False, first=True)
                with eng.Fori(1, LOOPS - 1) as i:
                    round_of_steps(i, k, g, with_chunks)
                round_of_steps(LOOPS - 1, k, g, with_chunks, final=True)
                part(trail, LOOPS - 1, k, g, LOOP_STEPS - 1)

            with eng.If(slow == 0):
                one_pass(k0, l * STEPS, True)
            with eng.Else():
                with eng.Fori(0, passes) as w:
                    one_pass(k0 + w * STEPS, 0, False)
                    if end_pass:
                        end_pass(l, w, k0 + w * STEPS + (STEPS - 1))
                if end_passes:
                    end_passes(l)
                if chunk_stage:
                    with eng.Fori(0, LOOPED) as c:
                        chunk_begin(l, c)
                        for j in range(LOOP_STEPS):
                            chunk_stage(l, j, c, last)
                    chunk_begin(l, LOOPED)
            if chunk_stage:
                for j in range(LOOP_STEPS):
                    chunk_stage(l, j, LOOPED, last)

        def parts(c):
            return LAST_PARTS if isinstance(c, int) and c == CHUNKS - 1 else CPART

        def chunk_rows(table, c, n=CPART):
            rows = table.rearrange("(c p j) f -> c p j f", p=CPART, j=4)
            return rows[bass.ds(c, 1), 0:n].rearrange("o p j f -> (o p) j f")

        enc_pq_ps = [pq_ps, sum_ps]

        def pq_view(ps, n=CPART):
            return ps[0:n, :].rearrange("p (j t f) -> p j t f", j=4, t=2)

        block = ctx.enter_context(nc.Block())

        @block.sync
        def _(sp):
            sp.dma_start(enc_wt_b[HID:128, :], io["enc_wt_b"]).then_inc(enc_in, 16)
            sp.dma_start(w1_nodes[HID:128], io["w1_nodes"]).then_inc(enc_in, 16)
            for q, (first, end) in enumerate(X_PIECES):
                piece = slice(first * CHUNK, end * CHUNK)
                sp.dma_start(state[HID:128, piece], io["x_t"][:, piece]).then_inc(x_in[q], 16)
                if q == 0:
                    sp.dma_start(dst_steps, io["dst_steps"]).then_inc(steps_in, 16)
            sp.dma_start(dst_i[:], io["dst"]).then_inc(dst_in, 16)
            sp.wait_ge(zeroed, 1)
            sp.dma_start(q_tab[0][NPAD:NWIN, :], zeros[0:WINDOW, 0:HID]).then_inc(zero_rows, 16)
            for l in range(1, LAYERS):
                sp.dma_start(q_tab[l][NLAST:NWIN, :].rearrange("(p j) f -> p j f", j=2),
                             zeros[0:(NWIN - NLAST) // 2, 0:2 * HID].rearrange("p (j f) -> p j f", j=2)).then_inc(zero_rows, 16)

            def enc_store(c, s):
                sp.wait_ge(enc_staged, done(c))
                settle(sp)
                sp.dma_start(chunk_rows(p_tab[0], c), stage[s][:, 0]).then_inc(stored[s], 16)
                sp.dma_start(chunk_rows(q_tab[0][0:NPAD, :], c), stage[s][:, 1]).then_inc(stored[s], 16)

            with sp.Fori(0, PAIRS) as i:
                for s in range(2):
                    enc_store(i * 2 + s, s)
            enc_store(CHUNKS - 1, 0)
            passes, slow = load_flags(sp)

            def lead(l, m, k, g, s):
                sp.wait_ge(added, slot_free(k, GATHER_SLOTS))
                settle(sp)
                sp.dma_start(idx[s][:], io["src"][bass.ds(m, 1)].rearrange("o p g -> (o p) g")).then_inc(idx_in[s], 16)

            def front(l, m, k, g, s):
                s = s % 2
                if isinstance(m, int) and m == 0:
                    all_stored(sp, l)
                sp.wait_ge(combined, slot_free(k))
                settle(sp)
                sp.dma_start(pick[s][WINDOW:FEATS, :], io["edge_t"][bass.ds(m, 1)].rearrange("o d e -> (o d) e")).then_inc(edge_in[s], 16)
                base = sp.value_load(base_i[0:1, bass.ds(m, 1)], min_val=0, max_val=NODES)
                sp.dma_start(source[0:WINDOW, l, s, :], q_tab[l][bass.ds(base, WINDOW), :]).then_inc(edge_in[s], 16)

            def end_pass(l, w, k):
                sp.sem_inc(pass_read, 1)
                sp.wait_ge(windows, (passes + 1) * l + w + 2)
                settle(sp)

            def end_passes(l):
                sp.wait_ge(windows, (passes + 1) * (l + 1) + 1)
                settle(sp)

            def chunk_begin(l, c):
                pass

            def chunk_stage(l, j, c, last):
                if l == LAYERS - 1 and j == 2:
                    sp.wait_ge(norm, c * NORM_OPS + 1)
                    settle(sp)
                    sp.dma_start(x_rows[0:parts(c)], chunk_rows(io["x_pad"], c, parts(c))).then_inc(xr_in, 16)

            sp.wait_ge(cleared, ONES)
            sp.wait_ge(zero_rows, 16 * LAYERS)
            for l in range(LAYERS):
                run_layer(sp, l, passes, slow, lead, front, None, None, chunk_begin, chunk_stage, end_pass, end_passes)

        @block.gpsimd
        def _(pool):
            nc.gpsimd.memset(ident[:], 1.0).then_inc(consts, 1)
            nc.gpsimd.iota(iota_i[:], pattern=[[1, WINDOW]], base=0, channel_multiplier=0)
            final = (LOOPS - 1) * LOOP_STEPS
            nc.gpsimd.iota(stair_i[:, 0:final], pattern=[[CHUNK, LOOPS - 1], [0, LOOP_STEPS]], base=0, channel_multiplier=0)
            nc.gpsimd.iota(stair_i[:, final:STEPS], pattern=[[CHUNK, 2], [0, HALF]], base=(LOOPS - 1) * CHUNK,
                           channel_multiplier=0)
            nc.gpsimd.iota(rungs_i[:], pattern=[[WINDOW, MAX_PASSES]], base=0, channel_multiplier=0)
            pool.wait_ge(consts, 1)
            nc.gpsimd.affine_select(out=ident[:], in_=ident[:], compare_op=ALU.is_equal, fill=0.0, base=0,
                                    pattern=[[-1, 128]], channel_multiplier=1).then_inc(consts, 1)
            pool.dma_start(enc_w[HID:128, :], io["enc_W"]).then_inc(weights_in, 16)
            pool.dma_start(enc_b[HID:128, :], io["enc_b"]).then_inc(weights_in, 16)
            pool.dma_start(w2t_b2[:], io["w2t_b2"]).then_inc(weights_in, 16)
            pool.dma_start(wih[:], io["wih"]).then_inc(weights_in, 16)
            pool.dma_start(bias_zr[:], io["bih"][0:128, :]).then_inc(weights_in, 16)
            pool.dma_start(bias_hzr[:], io["bhh"][0:128, :]).then_inc(weights_in, 16)
            pool.dma_start(bias_in[:], io["bih"][128:192, :]).then_inc(weights_in, 16)
            pool.dma_start(bias_hn[HID:128, :], io["bhh"][128:192, :]).then_inc(weights_in, 16)
            pool.wait_ge(reduced, 1)
            with nc.allow_non_contiguous_dma(reason="two numbers for each partition, once"):
                for k in range(2):
                    pool.dma_start(range_tab[k:k + 1, :].rearrange("o (p j) -> (o p) j", j=2),
                                   low_high[:, k, :]).then_inc(range_out, 16)
            pool.dma_start(ro_w1[HID:128, :], io["ro_W1"]).then_inc(weights_in, 16)
            pool.dma_start(ro_b1[:], io["ro_b1"]).then_inc(weights_in, 16)
            pool.wait_ge(range_out, 32)
            pool.dma_start(base_all[:], range_tab[0:1, :].to_broadcast([128, STEPS])).then_inc(range_in, 16)
            pool.dma_start(base_f[:], range_tab[0:1, :]).then_inc(range_in, 16)
            pool.dma_start(high_f[:], range_tab[1:2, :]).then_inc(range_in, 16)
            pool.dma_start(ro_w2b[:], io["ro_w2b"]).then_inc(weights_in, 16)
            for s in range(2):
                pool.dma_start(source[WINDOW:KEDGE, :, s, :], io["w1_edge"]).then_inc(weights_in, 16)
            pool.wait_ge(setup, 1)
            pool.dma_start(gate_w[HID:128, :, 0:2 * HID], io["whh"][:, :, 0:2 * HID]).then_inc(weights_in, 16)
            pool.dma_start(gate_w[HID:128, :, 3 * HID:4 * HID], io["whh"][:, :, 2 * HID:3 * HID]).then_inc(weights_in, 16)
            pool.wait_ge(consts, 2)
            ones = (pick[0][WINDOW:128, :], msg[0][:], pick[1][WINDOW:128, :], msg[1][:], hid[HID:HID + 1, :])
            for n, rows in enumerate(ones):
                if n:
                    pool.wait_ge(cleared, n)
                nc.gpsimd.memset(rows, 1.0).then_inc(cleared, 1)
            pool.wait_ge(cleared, ONES)
            nc.gpsimd.memset(sums[0:HID + 1, :], 0.0).then_inc(sums_clear, 1)
            passes, slow = load_flags(pool)

            def lead(l, m, k, g, s):
                pool.wait_ge(idx_in[s], arrivals(k, s, 16, GATHER_SLOTS))
                pool.wait_ge(added, slot_free(k, GATHER_SLOTS))
                settle(pool)
                for g in range(EDGE_TILES):
                    pool.indirect_dma_start(
                        out=p_src[s][:, g, :], out_offset=None, in_=p_tab[l][0:NODES, :],
                        in_offset=bass.IndirectOffsetOnAxis(ap=idx[s][:, g:g + 1], axis=0)).then_inc(gathered[s], 16)

            def end_pass(l, w, k):
                pool.wait_ge(added, done(k))
                settle(pool)
                pool.inc_swdge_sem(gathered, [16 * EDGE_TILES * STEPS // GATHER_SLOTS] * GATHER_SLOTS, mode="sub")
                pool.sem_inc(pass_read, 1)

            for l in range(LAYERS):
                all_stored(pool, l)
                run_layer(pool, l, passes, slow, lead, end_pass=end_pass)

        @block.tensor
        def _(pe):
            pe.sem_inc(enc_projected, CREDIT)
            pe.sem_inc(flipped, CREDIT)
            pe.sem_inc(combined, CREDIT)
            pe.sem_inc(scattered, CREDIT)
            pe.sem_inc(projected, 1)
            pe.sem_inc(hid_ps, 1)

            pe.wait_ge(enc_in, 32)
            nc.tensor.matmul(zr_ps[0:HID + 1, 0:2 * HID], enc_wt_b[HID:128, :], w1_nodes[HID:128, 0, :],
                             start=True, stop=True).then_inc(w1_ps, 1)
            pe.wait_ge(w1_sb, 1)

            def enc_project(c, s):
                pe.wait_ge(enc_x, done(c))
                pe.wait_ge(enc_staged, slot_free(c))
                xv = x_one[s][:].rearrange("q (p j) -> q j p", j=4)
                for j in range(4):
                    last = nc.tensor.matmul(enc_pq_ps[s][0:CPART, j * 128:(j + 1) * 128], xv[:, j, :],
                                            enc_w1[:], start=True, stop=True)
                last.then_inc(enc_projected, 1)

            with pe.Fori(0, PAIRS) as i:
                for s in range(2):
                    enc_project(i * 2 + s, s)
            enc_project(CHUNKS - 1, 0)
            pe.wait_ge(weights_in, 16 * WEIGHTS)
            for l in range(LAYERS):
                if l:
                    pe.wait_ge(vw_sb, l)
                nc.tensor.matmul(zr_ps[0:HID + 1, 0:3 * HID], w2t_b2[:, l, :], wih[:, l, :], start=True, stop=True).then_inc(vw_ps, 1)
            pe.wait_ge(vw_sb, LAYERS)
            pe.wait_ge(cleared, ONES)
            pe.wait_ge(consts, 2)
            pe.wait_ge(enc_staged, done(CHUNKS - 1))
            passes, slow = load_flags(pe)

            def lead(l, m, k, g, s):
                s = s % 2
                pe.wait_ge(hot_t_ready, done(k))
                pe.wait_ge(pick_ready, single_free(k))
                for g in range(EDGE_TILES):
                    last = nc.tensor.transpose(hott_ps[0:WINDOW, g * 128:(g + 1) * 128], hot_t[s][:, g, :], ident[:])
                last.then_inc(flipped, 1)

            def front(l, m, k, g, s):
                s = s % 2
                pe.wait_ge(pick_ready, done(k))
                pe.wait_ge(edge_in[s], arrivals(k, s, 32))
                pe.wait_ge(added, slot_free(k))
                for g in range(EDGE_TILES):
                    last = nc.tensor.matmul(pre_ps[s][:, g, :], pick[s][0:KEDGE, g * 128:(g + 1) * 128],
                                            source[0:KEDGE, l, s, :], start=True, stop=True)
                last.then_inc(combined, 1)

            def back(l, m, k, g, s):
                s = s % 2
                pe.wait_ge(hot_ready, done(k))
                pe.wait_ge(msg_ready, done(k))
                pe.wait_ge(summed, single_free(k))
                for g in range(EDGE_TILES):
                    last = nc.tensor.matmul(sum_ps[0:HID + 1, 0:WINDOW], msg[s][:, g, :], hot[s][:, g, :],
                                            start=(g == 0), stop=(g == EDGE_TILES - 1))
                last.then_inc(scattered, 1)

            def chunk_begin(l, c):
                n, w = before(l, c), 4 * parts(c)
                pe.wait_ge(chunk_h_in, n + 1)
                if l == LAYERS - 1:
                    pe.wait_ge(hid_ready, c + 1)
                if l == 0:
                    settle(pe)
                    nc.tensor.matmul(n_ps[HID:128, 0:w], enc_w[HID:128, :], chunk[HID:128, 0:w],
                                     start=True, stop=True).then_inc(enc_ps, 1)
                    pe.wait_ge(enc_h, c + 1)
                for ps, g in ((zr_ps, 0), (n_ps, 2 * HID)):
                    nc.tensor.matmul(ps[:, 0:w], gate_w[HID:128, l, g:g + 128], chunk[HID:128, 0:w], start=True, stop=False)

            def chunk_stage(l, j, c, last):
                n, w = before(l, c), 4 * parts(c)
                if j == 0:
                    pe.wait_ge(chunk_in, n + 1)
                    for ps, g in ((zr_ps, 0), (n_ps, 2 * HID)):
                        end = nc.tensor.matmul(ps[:, 0:w], sum_w[:, l, g:g + 128], chunk_sum[:, 0:w], start=False, stop=True)
                    end.then_inc(gates_ps, 1)
                if j == 3:
                    pe.wait_ge(gru, GRU_OPS * (n + 1) + 1)
                    if l < LAYERS - 1:
                        pe.wait_ge(staged, n + 1)
                        hn = h_next[:, 0:w].rearrange("q (p j) -> q j p", j=4)
                        for q in range(4):
                            end = nc.tensor.matmul(pq_ps[0:parts(c), q * 128:(q + 1) * 128], hn[HID:128, q, :],
                                                   w1_nodes[HID:128, l + 1, :], start=True, stop=True)
                        end.then_inc(projected, 1)
                    else:
                        settle(pe)
                        nc.tensor.matmul(zr_ps[0:HID, 0:w], ro_w1[HID:128, :], h_next[HID:128, 0:w],
                                         start=True, stop=True).then_inc(hid_ps, 1)
                if j == 4 and l == LAYERS - 1:
                    pe.wait_ge(hid_ready, c + 2)
                    pe.wait_ge(norm, c * NORM_OPS + 1)
                    hv = hid[:, 0:w].rearrange("q (p j) -> q j p", j=4)
                    for q in range(4):
                        end = nc.tensor.matmul(pq_ps[0:parts(c), q * HID:(q + 1) * HID], hv[:, q, :], ro_w2b[:],
                                               start=True, stop=True)
                    end.then_inc(y_ps, 1)

            for l in range(LAYERS):
                if l == LAYERS - 1:
                    pe.wait_ge(staged, CHUNKS * l + 1)
                run_layer(pe, l, passes, slow, lead, front, back, None, chunk_begin, chunk_stage)

        @block.scalar
        def _(act):
            act.sem_inc(enc_staged, CREDIT)
            act.wait_ge(w1_ps, 1)
            nc.scalar.copy(enc_w1[:], zr_ps[0:HID + 1, 0:2 * HID]).then_inc(w1_sb, 1)

            def enc_chunk(c, s, n_stored):
                act.wait_ge(enc_projected, done(c))
                if n_stored is not None:
                    act.wait_ge(stored[s], n_stored)
                nc.scalar.copy(stage[s][:].rearrange("p t j f -> p j t f"), pq_view(enc_pq_ps[s])).then_inc(enc_staged, 1)

            for c in range(2):
                enc_chunk(c, c, None)
            with act.Fori(1, PAIRS) as i:
                for s in range(2):
                    enc_chunk(i * 2 + s, s, i * 32)
            enc_chunk(CHUNKS - 1, 0, PAIRS * 32)
            act.wait_ge(setup, 1)
            for l in range(LAYERS):
                act.wait_ge(vw_ps, l + 1)
                nc.scalar.copy(sum_w[:, l, 0:3 * HID], zr_ps[0:HID + 1, 0:3 * HID]).then_inc(vw_sb, 1)
            passes, slow = load_flags(act)
            act.wait_ge(cleared, ONES)
            act.wait_ge(bias_ready, 1)
            for credit in (pick_ready, msg_ready):
                act.sem_inc(credit, CREDIT)
            for credit in (staged, h_kept, hid_ready):
                act.sem_inc(credit, 1)
            act.sem_inc(out_done, 16)

            def lead(l, m, k, g, s):
                s = s % 2
                act.wait_ge(flipped, done(k))
                act.wait_ge(combined, slot_free(k))
                nc.scalar.copy(pick[s][0:WINDOW, :], hott_ps[0:WINDOW, :]).then_inc(pick_ready, 1)

            def back(l, m, k, g, s):
                s = s % 2
                act.wait_ge(added, done(k))
                act.wait_ge(scattered, slot_free(k))
                nc.scalar.activation(msg[s][:, :, 0:HID], pre[s][:], ACT.Relu).then_inc(msg_ready, 1)

            def chunk_begin(l, c):
                n, w = before(l, c), 4 * parts(c)
                act.wait_ge(gru, n * GRU_OPS + 1)
                if l:
                    act.wait_ge(h_kept, CHUNKS * l + 1)
                settle(act)
                nc.scalar.copy(chunk[HID:128, 0:w], state[HID:128, bass.ds(c * CHUNK, w)]).then_inc(chunk_h_in, 1)

            def chunk_stage(l, j, c, last):
                n, w = before(l, c), 4 * parts(c)
                if j == 0:
                    act.wait_ge(summed, done(last))
                    settle(act)
                    nc.scalar.copy(chunk_sum[:, 0:w], sums[0:HID + 1, bass.ds(c * CHUNK, w)]).then_inc(chunk_in, 1)
                if j == 1:
                    act.wait_ge(gates_ps, n + 1)
                    nc.scalar.activation(zr[:, 0:w], zr_ps[:, 0:w], ACT.Sigmoid, bias=bias_zr[:, l:l + 1]).then_inc(zr_ready, 1)
                if j == 2:
                    act.wait_ge(gru, GRU_OPS * n + 4)
                    nc.scalar.activation(n_hi[HID:128, 0:w], npre[:, 0:w], ACT.Tanh, bias=bias_in[:, l:l + 1]).then_inc(n_ready, 1)
                if j == 3 and l < LAYERS - 1:
                    act.wait_ge(gru, GRU_OPS * (n + 1) + 1)
                    settle(act)
                    nc.scalar.copy(state[HID:128, bass.ds(c * CHUNK, w)], h_next[HID:128, 0:w]).then_inc(h_kept, 1)
                if j == 4 and l < LAYERS - 1:
                    act.wait_ge(projected, n + 2)
                    act.wait_ge(stored[0], stored_before(l, c))
                    nc.scalar.copy(stage[0][0:parts(c)].rearrange("p t j f -> p j t f"), pq_view(pq_ps, parts(c))).then_inc(staged, 1)
                    act.wait_ge(staged, n + 2)
                    act.dma_start(chunk_rows(p_tab[l + 1], c, parts(c)), stage[0][0:parts(c), 0]).then_inc(stored[0], 16)
                    act.dma_start(chunk_rows(q_tab[l + 1][0:NPAD, :], c, parts(c)), stage[0][0:parts(c), 1]).then_inc(stored[0], 16)
                if j == 4 and l == LAYERS - 1:
                    act.wait_ge(hid_ps, c + 2)
                    act.wait_ge(norm, c * NORM_OPS + 1)
                    nc.scalar.activation(hid[0:HID, 0:w], zr_ps[0:HID, 0:w], ACT.Relu, bias=ro_b1[:]).then_inc(hid_ready, 1)
                if j == 6 and l == LAYERS - 1:
                    act.wait_ge(norm, c * NORM_OPS + 8)
                    nc.scalar.activation(sd[0:parts(c)], veps[0:parts(c)], ACT.Sqrt).then_inc(sd_ready, 1)
                if j == 7 and l == LAYERS - 1:
                    act.wait_ge(norm, (c + 1) * NORM_OPS + 1)
                    if isinstance(c, int) and c == CHUNKS - 1:
                        whole = LAST_NODES // 64 * 16
                        rows = io["out"][c * CHUNK:NODES, :].rearrange("(p j) f -> p j f", j=4)
                        act.dma_start(rows[0:whole], y_out[0:whole]).then_inc(out_done, 16)
                        act.dma_start(rows[whole:], y_out[whole:LAST_NODES // 4]).then_inc(out_done, 16)
                    else:
                        act.dma_start(chunk_rows(io["out"][0:(CHUNKS - 1) * CHUNK, :], c), y_out[:]).then_inc(out_done, 16)

            for l in range(LAYERS):
                run_layer(act, l, passes, slow, lead, None, back, None, chunk_begin, chunk_stage)
            act.wait_ge(out_done, 16 * (CHUNKS + 2))

        @block.vector
        def _(dve):
            for credit in (enc_x, hot_t_ready, hot_ready, added, summed):
                dve.sem_inc(credit, CREDIT)
            dve.sem_inc(gru, 1)
            dve.sem_inc(norm, 1)
            nc.vector.memset(zeros[:], 0.0).then_inc(zeroed, 1)
            for s in range(2):
                last = nc.vector.memset(x_one[s][HID:HID + 1, :], 1.0)
            nc.vector.memset(gate_w[:], 0.0)
            nc.vector.memset(sum_w[:], 0.0).then_inc(setup, 1)

            def enc_chunk(c, s):
                dve.wait_ge(enc_projected, slot_free(c))
                nc.vector.tensor_copy(x_one[s][0:HID, :], state[HID:128, cols(c)]).then_inc(enc_x, 1)

            dve.wait_ge(x_in[0], 16)
            enc_chunk(0, 0)
            enc_chunk(1, 1)
            dve.wait_ge(steps_in, 16)
            nc.vector.tensor_reduce(low_high[:, 0, :], dst_steps, AX.X, ALU.min)
            dve.wait_ge(x_in[1], 16)
            enc_chunk(2, 0)
            enc_chunk(3, 1)
            nc.vector.tensor_reduce(low_high[:, 1, :], dst_steps, AX.X, ALU.max).then_inc(reduced, 1)
            with dve.Fori(2, X_PIECES[1][1] // 2) as i:
                for s in range(2):
                    enc_chunk(i * 2 + s, s)
            dve.wait_ge(x_in[2], 16)
            with dve.Fori(X_PIECES[1][1] // 2, SETUP_PAIR) as i:
                for s in range(2):
                    enc_chunk(i * 2 + s, s)

            chain = [1]

            def link(op):
                chain[0] += 1
                op.then_inc(setup, 1)
                dve.wait_ge(setup, chain[0])

            dve.wait_ge(consts, 2)
            nc.vector.tensor_copy(iota_ps, iota_i[:])
            nc.vector.tensor_copy(stair[:], stair_i[:])
            link(nc.vector.tensor_copy(rungs[:], rungs_i[:]))
            dve.wait_ge(dst_in, 16)
            dve.wait_ge(range_in, 48)
            nc.vector.tensor_copy(start_f[:], base_f[:])
            nc.vector.tensor_scalar(base_i[:], base_f[:], float(NODES), None, ALU.min)
            nc.vector.tensor_tensor(late[:], base_f[:], stair[:], ALU.is_lt)
            link(nc.vector.tensor_tensor(spread[:], high_f[:], base_f[:], ALU.subtract))
            nc.vector.tensor_reduce(late_n[:], late[:], AX.X, ALU.add)
            link(nc.vector.tensor_reduce(widest[:], spread[:], AX.X, ALU.max))
            link(nc.vector.tensor_scalar(reach[:], rungs[:], widest[0:1, 0:1], None, ALU.is_le))
            link(nc.vector.tensor_reduce(passes_f[:], reach[:], AX.X, ALU.add))
            link(nc.vector.scalar_tensor_tensor(slow_f[:], passes_f[:], -1.0, late_n[:], ALU.add, ALU.add))
            nc.vector.tensor_copy(flags[0:1, 0:1], passes_f[:])
            nc.vector.tensor_copy(flags[0:1, 1:2], slow_f[:]).then_inc(windows, 1)

            with dve.Fori(SETUP_PAIR, PAIRS) as i:
                for s in range(2):
                    enc_chunk(i * 2 + s, s)
            enc_chunk(CHUNKS - 1, 0)
            nc.vector.tensor_tensor(rel[:], dst_i[:], base_all[:].unsqueeze(2).to_broadcast([128, STEPS, EDGE_TILES]), ALU.subtract)
            dve.wait_ge(weights_in, 16 * WEIGHTS)
            nc.vector.tensor_tensor(bias_zr[:], bias_zr[:], bias_hzr[:], ALU.add).then_inc(bias_ready, 1)
            dve.wait_ge(sums_clear, 1)
            dve.wait_ge(bias_ready, 1)
            passes, slow = load_flags(dve)

            def rel_of(m):
                return rel[:, bass.ds(m, 1), :].rearrange("p o g -> p (o g)").unsqueeze(2).to_broadcast([128, EDGE_TILES, WINDOW])

            node = iota_ps.unsqueeze(1).to_broadcast([128, EDGE_TILES, WINDOW])

            def lead(l, m, k, g, s):
                s = s % 2
                dve.wait_ge(flipped, slot_free(k))
                nc.vector.tensor_tensor(hot_t[s][:], rel_of(m), node, ALU.is_equal).then_inc(hot_t_ready, 1)

            def front(l, m, k, g, s):
                s = s % 2
                dve.wait_ge(scattered, slot_free(k))
                nc.vector.tensor_tensor(hot[s][:], rel_of(m), node, ALU.is_equal).then_inc(hot_ready, 1)

            def back(l, m, k, g, s):
                r, s = s, s % 2
                dve.wait_ge(gathered[r], arrivals(g, r, 16 * EDGE_TILES, GATHER_SLOTS))
                dve.wait_ge(combined, done(k))
                dve.wait_ge(msg_ready, slot_free(k))
                nc.vector.tensor_tensor(pre[s][:], pre_ps[s][:], p_src[r][:], ALU.add).then_inc(added, 1)

            def trail(l, m, k, g, s):
                base = dve.value_load(base_i[0:1, bass.ds(m, 1)], min_val=0, max_val=NODES)
                dve.wait_ge(scattered, done(k))
                dve.wait_ge(summed, single_free(k))
                here = bass.ds(base, WINDOW)
                nc.vector.tensor_tensor(sums[0:HID + 1, here], sum_ps[0:HID + 1, 0:WINDOW], sums[0:HID + 1, here],
                                        ALU.add).then_inc(summed, 1)

            def end_pass(l, w, k):
                dve.wait_ge(hot_ready, done(k))
                dve.wait_ge(pass_read, (passes * l + w + 1) * 2)
                nc.vector.tensor_scalar(rel[:], rel[:], float(-WINDOW), None, ALU.add)
                nc.vector.tensor_scalar(start_f[:], start_f[:], float(WINDOW), None, ALU.add).then_inc(window_step, 1)
                dve.wait_ge(window_step, (passes + 1) * l + w + 1)
                nc.vector.tensor_scalar(base_i[:], start_f[:], float(NODES), None, ALU.min).then_inc(windows, 1)
                dve.wait_ge(windows, (passes + 1) * l + w + 2)
                settle(dve)

            def end_passes(l):
                nc.vector.tensor_tensor(rel[:], dst_i[:], base_all[:].unsqueeze(2).to_broadcast([128, STEPS, EDGE_TILES]), ALU.subtract)
                nc.vector.tensor_copy(start_f[:], base_f[:]).then_inc(window_step, 1)
                nc.vector.tensor_scalar(base_i[:], base_f[:], float(NODES), None, ALU.min).then_inc(windows, 1)
                dve.wait_ge(windows, (passes + 1) * (l + 1) + 1)
                settle(dve)

            def chunk_begin(l, c):
                w = 4 * parts(c)
                if l == 0:
                    dve.wait_ge(enc_ps, c + 1)
                    nc.vector.tensor_scalar(chunk[HID:128, 0:w], n_ps[HID:128, 0:w], enc_b[HID:128, :], None,
                                            ALU.add).then_inc(enc_h, 1)

            def chunk_stage(l, j, c, last):
                n, w = before(l, c), 4 * parts(c)
                g0 = GRU_OPS * n + 1
                if j == 1:
                    dve.wait_ge(chunk_in, n + 1)
                    dve.wait_ge(summed, done(last))
                    nc.vector.tensor_copy(sums[0:HID + 1, bass.ds(c * CHUNK, w)], zeros[0:HID + 1, 0:w]).then_inc(gru, 1)
                    dve.wait_ge(zr_ready, n + 1)
                    nc.vector.scalar_tensor_tensor(rn[:, 0:w], n_ps[HID:128, 0:w], bias_hn[HID:128, l:l + 1], zr[HID:128, 0:w],
                                                   ALU.add, ALU.mult).then_inc(gru, 1)
                    dve.wait_ge(gru, g0 + 2)
                    nc.vector.tensor_tensor(npre[:, 0:w], n_ps[0:HID, 0:w], rn[:, 0:w], ALU.add).then_inc(gru, 1)
                if j == 2:
                    dve.wait_ge(n_ready, n + 1)
                    nc.vector.tensor_tensor(diff[:, 0:w], chunk[HID:128, 0:w], n_hi[HID:128, 0:w], ALU.subtract).then_inc(gru, 1)
                    dve.wait_ge(gru, g0 + 4)
                    nc.vector.tensor_tensor(zdiff[HID:128, 0:w], zr[0:HID, 0:w], diff[:, 0:w], ALU.mult).then_inc(gru, 1)
                    dve.wait_ge(gru, g0 + 5)
                    if l < LAYERS - 1:
                        dve.wait_ge(projected, n + 1)
                        dve.wait_ge(h_kept, n + 1)
                    else:
                        dve.wait_ge(hid_ps, c + 1)
                    nc.vector.tensor_tensor(h_next[HID:128, 0:w], n_hi[HID:128, 0:w], zdiff[HID:128, 0:w], ALU.add).then_inc(gru, 1)
                if j == 5 and l == LAYERS - 1:
                    n0, p = c * NORM_OPS + 1, parts(c)
                    dve.wait_ge(y_ps, c + 1)
                    dve.wait_ge(xr_in, c * 16 + 16)
                    nc.vector.tensor_tensor(y[0:p], pq_ps[0:p, 0:4 * HID].rearrange("p (j f) -> p j f", j=4), x_rows[0:p], ALU.add).then_inc(norm, 1)
                    dve.wait_ge(norm, n0 + 1)
                    nc.vector.tensor_reduce(ysum[0:p], y[0:p], AX.X, ALU.add).then_inc(norm, 1)
                    dve.wait_ge(norm, n0 + 2)
                    nc.vector.tensor_scalar(ymean[0:p], ysum[0:p], 1.0 / HID, None, ALU.mult).then_inc(norm, 1)
                    dve.wait_ge(norm, n0 + 3)
                    nc.vector.tensor_tensor(yc[0:p], y[0:p], ymean[0:p].unsqueeze(2).to_broadcast([p, 4, HID]), ALU.subtract).then_inc(norm, 1)
                    dve.wait_ge(norm, n0 + 4)
                    nc.vector.tensor_tensor(ysq[0:p], yc[0:p], yc[0:p], ALU.mult).then_inc(norm, 1)
                    dve.wait_ge(norm, n0 + 5)
                    nc.vector.tensor_reduce(vsum[0:p], ysq[0:p], AX.X, ALU.add).then_inc(norm, 1)
                    dve.wait_ge(norm, n0 + 6)
                    nc.vector.tensor_scalar(veps[0:p], vsum[0:p], 1.0 / HID, EPS, ALU.mult, ALU.add).then_inc(norm, 1)
                if j == 6 and l == LAYERS - 1:
                    n0, p = c * NORM_OPS + 1, parts(c)
                    dve.wait_ge(sd_ready, c + 1)
                    nc.vector.reciprocal(rstd[0:p], sd[0:p]).then_inc(norm, 1)
                    dve.wait_ge(norm, n0 + 8)
                    dve.wait_ge(out_done, c * 16 + 16)
                    nc.vector.tensor_tensor(y_out[0:p], yc[0:p], rstd[0:p].unsqueeze(2).to_broadcast([p, 4, HID]), ALU.mult).then_inc(norm, 1)

            for l in range(LAYERS):
                if l:
                    dve.wait_ge(gru, GRU_OPS * CHUNKS * l + 1)
                run_layer(dve, l, passes, slow, lead, front, back, trail, chunk_begin, chunk_stage, end_pass, end_passes)


def kernel(**inputs):
    import numpy as np
    import concourse.bacc as bacc
    from concourse.bass_utils import run_bass_kernel_spmd

    a = {k.replace("L0_gnn_", ""): np.asarray(v) for k, v in inputs.items()}
    padded = STEPS * STEP

    def pad(v, n, fill=0):
        out = np.full((n,) + v.shape[1:], fill, v.dtype)
        out[:len(v)] = v
        return out

    src = pad(a["src"], padded).reshape(STEPS, EDGE_TILES, 128)
    dst = pad(a["dst"], padded, NODES)
    edge = pad(a["edge_attr_16"], padded)
    x = pad(a["x"], NPAD)

    def gates(v):
        return v.reshape(v.shape[:-1] + (3, HID))[..., [1, 0, 2], :].reshape(v.shape)

    w1 = a["msg_W1"]
    arrays = {
        "x_t": x.T,
        "x_pad": x,
        "src": src.transpose(0, 2, 1),
        "dst": dst.reshape(STEPS, EDGE_TILES, 128).transpose(2, 0, 1),
        "dst_steps": dst.reshape(STEPS // 2, 2, STEP),
        "edge_t": edge.reshape(STEPS, STEP, EDGE_DIM).transpose(0, 2, 1),
        "enc_W": a["enc_W"],
        "enc_wt_b": np.concatenate([a["enc_W"].T, a["enc_b"][:, None]], 1),
        "enc_b": a["enc_b"][:, None],
        "w1_nodes": np.concatenate([w1[:, :HID], w1[:, HID:2 * HID]], 2).transpose(1, 0, 2),
        "w1_edge": np.concatenate([w1[:, 2 * HID:], a["msg_b1"][:, None]], 1).transpose(1, 0, 2),
        "w2t_b2": np.concatenate([a["msg_W2"], a["msg_b2"][:, None]], 1).transpose(2, 0, 1),
        "wih": gates(a["gru_Wih"]).transpose(1, 0, 2),
        "whh": gates(a["gru_Whh"]).transpose(1, 0, 2),
        "bih": gates(a["gru_bih"]).T,
        "bhh": gates(a["gru_bhh"]).T,
        "ro_W1": a["ro_W1"],
        "ro_b1": a["ro_b1"][:, None],
        "ro_w2b": np.concatenate([a["ro_W2"], a["ro_b2"][None]], 0),
    }
    nc = bacc.Bacc("TRN2", target_bir_lowering=False, num_devices=1)
    io = {}
    for name, v in arrays.items():
        arrays[name] = v = np.ascontiguousarray(v)
        dt = U32 if name == "src" else I32 if name.startswith("dst") else F32
        if name == "src":
            arrays[name] = v = v.view(np.uint32)
        io[name] = nc.dram_tensor(f"in_{name}", v.shape, dt, kind="ExternalInput").ap()
    io["out"] = nc.dram_tensor("out", (NODES, HID), F32, kind="ExternalOutput").ap()
    build(nc, io)
    result = run_bass_kernel_spmd(nc, [{f"in_{k}": v for k, v in arrays.items()}], core_ids=[0])
    return result.results[0]["out"]
```
